# Optimizing a Trainium2 kernel written in Bass

```python
import numpy as np
import jax
import jax.numpy as jnp

def _softmax(x, axis=-1):
    return jax.nn.softmax(x, axis=axis)

def _gelu(x):
    return jax.nn.gelu(x, approximate=True)

def _silu(x):
    return jax.nn.silu(x)

def _sigmoid(x):
    return jax.nn.sigmoid(x)

def _layernorm(x, axis=-1, eps=1e-05):
    m = jnp.mean(x, axis=axis, keepdims=True)
    v = jnp.var(x, axis=axis, keepdims=True)
    return (x - m) / jnp.sqrt(v + eps)

def _scatter_add(tgt, idx, src, axis=0):
    return tgt.at[idx].add(src)

def _segment_sum(src, seg, n):
    return jax.ops.segment_sum(src, seg, n)
kernel_name = 'mk_adj_preln_d1_adj_r2_e0acf6'

def setup_inputs(seed: int=0):
    np.random.seed(seed)
    _w = jnp.asarray

    def _rec_inputs():
        import jax
        import jax.numpy as jnp
        _gk = jax.random.key(seed)
        x = -0.0002928 + 1 * jax.random.normal(jax.random.fold_in(_gk, 1), (8, 1024, 256), jnp.float32)
        _w = (1.0 + jnp.arange(1024, dtype=jnp.float32)) ** (-0.5)
        _w = _w / _w.mean()
        _pij = jnp.clip(0.0078125 * _w[:, None] * _w[None, :], 0.0, 1.0)
        _a = jax.random.uniform(jax.random.fold_in(_gk, 2), (1024, 1024)) < _pij
        _af = _a.astype(jnp.float32)
        adj = _af
        return (x, adj)
    x, adj = _rec_inputs()

    def _L0_gnn_setup():
        import jax, jax.numpy as jnp
        import numpy as np
        B, N, D, H = (4, 1024, 256, 8)
        HD = D // H
        key = jax.random.key(seed)
        ks = jax.random.split(key, 10)
        x = jax.random.normal(ks[0], (B, N, D), dtype=jnp.float32)
        adj = (jax.random.uniform(ks[1], (N, N)) < 0.1).astype(jnp.float32)
        s = 1.0 / np.sqrt(D)
        Wq = jax.random.normal(ks[2], (D, D), dtype=jnp.float32) * s
        Wk = jax.random.normal(ks[3], (D, D), dtype=jnp.float32) * s
        Wv = jax.random.normal(ks[4], (D, D), dtype=jnp.float32) * s
        Wo = jax.random.normal(ks[5], (D, D), dtype=jnp.float32) * s
        bq = jnp.zeros((D,), jnp.float32)
        bk = jnp.zeros((D,), jnp.float32)
        bv = jnp.zeros((D,), jnp.float32)
        bo = jnp.zeros((D,), jnp.float32)
        return {'x': x, 'adj': adj, 'Wq': Wq, 'bq': bq, 'Wk': Wk, 'bk': bk, 'Wv': Wv, 'bv': bv, 'Wo': Wo, 'bo': bo}
    _L0_gnn_all = _L0_gnn_setup()
    _L0_gnn_in = {k: v for k, v in _L0_gnn_all.items() if k in ('Wq', 'bq', 'Wk', 'bk', 'Wv', 'bv', 'Wo', 'bo')}
    del _L0_gnn_all
    return {'x': x, 'adj': adj, 'L0_gnn_Wq': _L0_gnn_in['Wq'], 'L0_gnn_bq': _L0_gnn_in['bq'], 'L0_gnn_Wk': _L0_gnn_in['Wk'], 'L0_gnn_bk': _L0_gnn_in['bk'], 'L0_gnn_Wv': _L0_gnn_in['Wv'], 'L0_gnn_bv': _L0_gnn_in['bv'], 'L0_gnn_Wo': _L0_gnn_in['Wo'], 'L0_gnn_bo': _L0_gnn_in['bo']}

def reference(x, adj, L0_gnn_Wq, L0_gnn_bq, L0_gnn_Wk, L0_gnn_bk, L0_gnn_Wv, L0_gnn_bv, L0_gnn_Wo, L0_gnn_bo):
    import jax
    import jax.numpy as jnp

    def _L0_gnn_ref(x, adj, Wq, bq, Wk, bk, Wv, bv, Wo, bo):
        import jax, jax.numpy as jnp
        import numpy as np
        B, N, D, H = (4, 1024, 256, 8)
        HD = D // H
        b, n, d = x.shape
        q = (x @ Wq + bq).reshape(b, n, H, HD)
        k = (x @ Wk + bk).reshape(b, n, H, HD)
        v = (x @ Wv + bv).reshape(b, n, H, HD)
        scores = jnp.einsum('bqhd,bkhd->bhqk', q, k) / jnp.sqrt(jnp.float32(HD))
        scores = scores + (1.0 - adj)[None, None, :, :] * -1000000000.0
        attn = jax.nn.softmax(scores, axis=-1)
        out = jnp.einsum('bhqk,bkhd->bqhd', attn, v).reshape(b, n, d)
        return out @ Wo + bo
    h = jnp.maximum(_layernorm(x, axis=-1), 0.0)
    x = x + _L0_gnn_ref(h, adj, L0_gnn_Wq, L0_gnn_bq, L0_gnn_Wk, L0_gnn_bk, L0_gnn_Wv, L0_gnn_bv, L0_gnn_Wo, L0_gnn_bo)
    return x

_drawn_inputs = setup_inputs


def setup_inputs(seed=0):
    import zlib

    import numpy as np

    out = dict(_drawn_inputs(seed))
    spreads = {'L0_gnn_bq': (0.0, 0.701),
     'L0_gnn_bk': (0.0, 0.8),
     'L0_gnn_bv': (0.0, 0.1),
     'L0_gnn_bo': (0.0, 0.1)}
    factors = {}
    for name, (base, spread) in spreads.items():
        noise = np.random.default_rng([zlib.crc32(name.encode()), seed]).standard_normal(out[name].shape)
        drawn = base * np.exp(spread * noise) if base else spread * noise
        out[name] = jnp.asarray(drawn.astype(out[name].dtype))
    for name, factor in factors.items():
        out[name] = (out[name] * factor).astype(out[name].dtype)
    return out
```

```python
from contextlib import ExitStack

import concourse.bass as bass
from concourse import mybir

F32 = mybir.dt.float32
F32R = mybir.dt.float32r
ALU = mybir.AluOpType
ACT = mybir.ActivationFunctionType

P = 128
BANK = 512
BATCH, TOKENS, DIM, HEADS = 8, 1024, 256, 8
HEAD_DIM = DIM // HEADS
PARTS = P // HEAD_DIM
PHASES = HEADS // PARTS
TILES = TOKENS // P
DCH = DIM // P
CHUNKS = TOKENS // BANK
UNIT_TILES = 2
UNIT_Q = UNIT_TILES * P
UNIT_ROWS = UNIT_TILES * PARTS
UNITS = TILES // UNIT_TILES
ROWS = UNITS * UNIT_ROWS
BATCH_ROWS = PHASES * ROWS
BATCH_UNITS = PHASES * UNITS
RING = 4

EPS = 1e-5
MASKED = 1e9
START_MIN = 3.0e38

QK_STEPS = 2 * CHUNKS
V_STEPS = TILES * P // BANK
HT_STEPS = DCH * CHUNKS
PREP_STEPS = HT_STEPS + QK_STEPS + V_STEPS
BATCH_STEPS = HT_STEPS + 2 * (QK_STEPS + V_STEPS) + BATCH_UNITS + UNITS
STACK_DMAS = 2 * PARTS * PARTS

QK_SLOTS = {0: (0, 0), 1: (0, 1), 2: (1, 0), 3: (1, 1), 4: (2, 0), 5: (2, 1), 8: (3, 0), 9: (3, 1)}
V_SLOTS = ({10: (0, 0), 11: (0, 1), 12: (1, 0), 13: (1, 1)},
           {12: (0, 0), 13: (0, 1), 16: (1, 0), 17: (1, 1)})
HT_SLOTS = {24: 0, 25: 1, 26: 2, 27: 3}
O_SLOTS = {10: (0, 0), 11: (0, 1), 18: (1, 0), 19: (1, 1), 26: (2, 0), 27: (2, 1)}
NORM_ROW = 1
STATS_SLOT = 10


def gnn_kernel(nc, x, adj, Wq, bq, Wk, bk, Wv, bv, Wo, bo, out):
    SCALE = float(HEAD_DIM) ** -0.5
    x_v = x.rearrange("b (t p) d -> b p t d", p=P)
    out_v = out.rearrange("b (t p) d -> b p t d", p=P)
    adj_v = adj.rearrange("(t p) k -> p t k", p=P)

    with ExitStack() as ctx:
        def sb(name, shape, dt=F32):
            return ctx.enter_context(nc.sbuf_tensor(name, shape, dt))

        def pb(name, shape, dt=F32):
            return ctx.enter_context(nc.psum_tensor(name, shape, dt))

        def sem(name):
            return ctx.enter_context(nc.semaphore(name))

        mask = sb("mask", [P, TILES, TOKENS])
        q_stack = [sb(f"q_stack{g}", [P, PARTS, TOKENS], F32R) for g in range(PHASES)]
        k_stack = [sb(f"k_stack{g}", [P, PARTS, TOKENS], F32R) for g in range(PHASES)]
        rows = sb("rows", [P, RING, TOKENS])
        turned_p = sb("turned_p", [P, PARTS, TILES, UNIT_Q])
        hi = [sb(f"{n}_hi", [P, TOKENS], F32R) for n in "qk"]
        lo = [sb(f"{n}_lo", [P, TOKENS], F32R) for n in "qk"]
        ht = sb("ht", [P, DCH, TOKENS])
        xn = sb("xn", [P, TILES, DIM])
        v = [sb(f"v{g}", [P, TILES, P]) for g in range(PHASES)]
        w = {n: sb(f"w{n}", [P, DCH, DIM]) for n in "qkvo"}
        heads_t = [sb("heads_t0", [P, TOKENS]), sb("heads_t1", [P, 2, UNIT_Q])]
        res = sb("res", [P, 2, UNIT_TILES, DIM])
        inv_wide = sb("inv_wide", [P, UNIT_TILES, PARTS, HEAD_DIM])
        inv_t = sb("inv_t", [P, UNIT_Q])
        ident = sb("ident", [P, P])
        bv_row = sb("bv_row", [P, DIM])
        bo_row = sb("bo_row", [P, DIM])
        bias = {n: sb(f"b{n}_col", [P, PHASES]) for n in "qk"}
        row_min = sb("row_min", [P, RING])
        row_sum = sb("row_sum", [P, 2, UNIT_ROWS])
        row_inv = sb("row_inv", [P, UNIT_ROWS])
        stats = sb("stats", [P, TILES, 6])
        mean_var = sb("mean_var", [P, TILES, 2])
        ln = {n: sb(f"ln_{n}", [P, TILES]) for n in ("neg_mean", "var", "power", "rstd", "t0", "t1", "t2")}

        ps_scores = [pb(f"ps_scores{i}", [P, TOKENS]) for i in range(2)]
        ps_turn = [pb(f"ps_turn{i}", [P, PARTS, P]) for i in range(2)]
        ps_heads = pb("ps_heads", [P, BANK])
        ps_side = pb("ps_side", [P, BANK])

        START = 1
        weights_in = sem("weights_in")
        mask_in = sem("mask_in")
        x_in = sem("x_in")
        res_in = [sem(f"res_in{i}") for i in range(2)]
        stacked = [sem(f"stacked{g}") for g in range(PHASES)]
        out_stored = sem("out_stored")
        weights_ready = sem("weights_ready")
        mask_ready = sem("mask_ready")
        ident_ready = sem("ident_ready")
        stats_done = sem("stats_done")
        moments_done = sem("moments_done")
        ln_chain = sem("ln_chain")
        normed = sem("normed")
        scores_done = sem("scores_done")
        masked = sem("masked")
        exp_done = sem("exp_done")
        turn_a = sem("turn_a")
        turn_b = sem("turn_b")
        copied_a = sem("copied_a")
        copied_b = sem("copied_b")
        heads_done = sem("heads_done")
        inv_done = sem("inv_done")
        inv_spread = sem("inv_spread")
        inv_turned = sem("inv_turned")
        inv_copied = sem("inv_copied")
        heads_normed = sem("heads_normed")
        ht_turned = sem("ht_turned")
        ht_done = sem("ht_done")
        qk_done = sem("qk_done")
        hi_done = sem("hi_done")
        lo_done = sem("lo_done")
        v_done = sem("v_done")
        v_ready = sem("v_ready")
        o_done = sem("o_done")
        res_ready = sem("res_ready")
        out_ready = sem("out_ready")

        def row(b, g, i):
            return b * BATCH_ROWS + (g * ROWS + i)

        def unit(b, g, u):
            return b * BATCH_UNITS + (g * UNITS + u)

        def ahead(g, i, k):
            return g * ROWS + i + k

        def qk_step(b, g, s):
            return b * (2 * QK_STEPS) + (g * QK_STEPS + s)

        def v_step(b, g, s):
            return b * (2 * V_STEPS) + (g * V_STEPS + s)

        order = []
        for g in range(PHASES):
            for i in range(ROWS):
                if i in QK_SLOTS and QK_SLOTS[i][1] == 0:
                    order.append(("qk", g, QK_SLOTS[i][0]))
                if i in V_SLOTS[g] and V_SLOTS[g][i][1] == 0:
                    order.append(("v", g, V_SLOTS[g][i][0]))
                if g == 0 and i in HT_SLOTS:
                    order.append(("ht", g, HT_SLOTS[i]))
                if g == 1 and i in O_SLOTS and O_SLOTS[i][1] == 0:
                    order.append(("o", g, O_SLOTS[i][0]))
                if i % UNIT_ROWS == UNIT_ROWS - 1:
                    order.append(("inv", g, i // UNIT_ROWS))
        order.append(("o", 1, UNITS - 1))
        assert len(order) == BATCH_STEPS

        def held(eng, count):
            return count if isinstance(count, int) else eng.snap(eng.to_reg(count))

        def batches(eng, body):
            with eng.Fori(0, BATCH - 1) as b:
                body(b, False)
            body(BATCH - 1, True)

        block = ctx.enter_context(nc.Block())

        @block.sync
        def _(sp):
            def load_x(b):
                sp.dma_start(xn[:], x_v[b]).then_inc(x_in, 16)

            def load_res(b, u):
                sp.dma_start(res[:, u % 2], x_v[b, :, u * UNIT_TILES:(u + 1) * UNIT_TILES, :]
                             ).then_inc(res_in[u % 2], 16)

            def stack(bg, g, rows_before):
                if rows_before is not None:
                    sp.wait_ge(scores_done, rows_before)
                for t, dst, parts in ((0, q_stack[g], (hi[0], lo[0], hi[0], lo[0])),
                                      (1, k_stack[g], (hi[1], hi[1], lo[1], lo[1]))):
                    sp.wait_ge(lo_done, qk_step(bg, g, QK_STEPS - 2 + t) + 1)
                    for r in range(PARTS):
                        for h in range(PARTS):
                            sp.dma_start(dst[r * HEAD_DIM:(r + 1) * HEAD_DIM, h, :].bitcast(F32),
                                         parts[r][h * HEAD_DIM:(h + 1) * HEAD_DIM, :].bitcast(F32)
                                         ).then_inc(stacked[g], 16)

            load_x(0)
            for n, src in zip("qkvo", (Wq, Wk, Wv, Wo)):
                sp.dma_start(w[n][:], src.rearrange("(c p) n -> p c n", p=P)).then_inc(weights_in, 16)
            for n, src in zip("qk", (bq, bk)):
                sp.dma_start(bias[n][:], src.rearrange("(g p) -> p g", p=P), allow_slow_non_contiguous=True).then_inc(weights_in, 16)
            for row_t, src in ((bv_row, bv), (bo_row, bo)):
                sp.dma_start(row_t[:], src.partition_broadcast(P)).then_inc(weights_in, 16)
            sp.dma_start(mask[:], adj_v).then_inc(mask_in, 16)
            load_res(0, 0)
            load_res(0, 1)
            stack(0, 0, None)

            def body(b, last):
                if not last:
                    sp.wait_ge(ht_turned, b * HT_STEPS + HT_STEPS)
                    load_x(b + 1)
                stack(b, 1, row(b, 0, 0) + 1)

                if not last:
                    stack(b + 1, 0, row(b, 1, 0))
                for u in range(UNITS):
                    sp.wait_ge(out_ready, b * UNITS + (u + 1))
                    sp.dma_start(out_v[b, :, u * UNIT_TILES:(u + 1) * UNIT_TILES, :], res[:, u % 2]
                                 ).then_inc(out_stored, 16)
                    if u + 2 < UNITS or not last:
                        sp.wait_ge(out_stored, (b * UNITS + (u + 1)) * 16)
                        load_res(*((b, u + 2) if u + 2 < UNITS else (b + 1, u + 2 - UNITS)))

            batches(sp, body)
            sp.wait_ge(out_stored, BATCH * UNITS * 16)

        @block.gpsimd
        def _(pool):
            pool.sem_inc(inv_spread, START)
            pool.memset(ident[:], 0.0).then_inc(turn_b, RING)
            pool.wait_ge(turn_b, RING)
            pool.affine_select(out=ident[:], in_=ident[:], compare_op=ALU.not_equal, fill=1.0, base=0,
                               pattern=[[-1, P]], channel_multiplier=1).then_inc(ident_ready, 1)
            pool.memset(ln["power"][:], -0.5).then_inc(ln_chain, 1)
            pool.wait_ge(weights_in, 8 * 16)

            LN_STEPS = 7

            def own():
                pool.wait_ge(ident_ready, 1)

            def norm(b):
                base = b * LN_STEPS + 1
                count = held(pool, b * TILES + TILES)
                own()
                pool.wait_ge(moments_done, count)
                mean, var = mean_var[:, :, 0], mean_var[:, :, 1]
                pool.tensor_scalar(ln["neg_mean"][:], mean, -1.0, None, ALU.mult).then_inc(ln_chain, 1)
                pool.tensor_scalar(ln["var"][:], var, EPS, None, ALU.add).then_inc(ln_chain, 1)
                pool.wait_ge(ln_chain, base + 2)
                pool.tensor_tensor(ln["t0"][:], ln["var"][:], ln["power"][:], ALU.pow).then_inc(ln_chain, 1)
                pool.wait_ge(ln_chain, base + 3)
                pool.tensor_tensor(ln["t1"][:], ln["t0"][:], ln["t0"][:], ALU.mult).then_inc(ln_chain, 1)
                pool.wait_ge(ln_chain, base + 4)
                pool.tensor_tensor(ln["t2"][:], ln["t1"][:], ln["var"][:], ALU.mult).then_inc(ln_chain, 1)
                count = held(pool, base + 5)
                own()
                pool.wait_ge(ln_chain, count)
                pool.tensor_scalar(ln["t1"][:], ln["t2"][:], -0.5, 1.5, ALU.mult, ALU.add).then_inc(ln_chain, 1)
                pool.wait_ge(ln_chain, base + 6)
                pool.tensor_tensor(ln["rstd"][:], ln["t0"][:], ln["t1"][:], ALU.mult).then_inc(ln_chain, 1)
                count = held(pool, base + 7)
                own()
                pool.wait_ge(ln_chain, count)
                for t in range(TILES):
                    pool.tensor_scalar(xn[:, t, :], xn[:, t, :], ln["neg_mean"][:, t:t + 1],
                                       ln["rstd"][:, t:t + 1], ALU.add, ALU.mult).then_inc(normed, 1)

            norm(0)

            def body(b, last):
                for g in range(PHASES):
                    for u in range(UNITS):
                        count = held(pool, unit(b, g, u) + 1)
                        own()
                        pool.wait_ge(inv_done, count)
                        pool.wait_ge(inv_turned, count)
                        pool.tensor_copy(inv_wide[:], row_inv[:].rearrange("p (t h) -> p t h", h=PARTS)
                                         .unsqueeze(3).to_broadcast([P, UNIT_TILES, PARTS, HEAD_DIM])
                                         ).then_inc(inv_spread, 1)
                        if g == 0 and u == 1 and not last:
                            norm(b + 1)
                        if g == 0 and u == 3 or g == 1 and u < UNITS - 1:
                            k = 0 if g == 0 else u + 1
                            pool.wait_ge(res_in[k % 2], (b * (UNITS // 2) + (k // 2 + 1)) * 16)
                            pool.tensor_tensor(res[:, k % 2], res[:, k % 2],
                                               bo_row[:].unsqueeze(1).to_broadcast([P, UNIT_TILES, DIM]),
                                               ALU.add).then_inc(res_ready, 1)

            batches(pool, body)

        @block.scalar
        def _(act):
            def exp(m, n):
                act.wait_ge(masked, n + 1)
                u, j = m // UNIT_ROWS, m % UNIT_ROWS
                nc.scalar.activation(rows[:, m % RING, :], rows[:, m % RING, :], ACT.Exp,
                                     bias=row_min[:, m % RING:m % RING + 1], scale=-1.0,
                                     accum_out=row_sum[:, u % 2, j:j + 1]).then_inc(exp_done, 1)

            def copy_a(b, g, i):
                act.wait_ge(turn_a, row(b, g, i) + 1)
                t, h = i // PARTS % UNIT_TILES, i % PARTS
                nc.scalar.activation(turned_p[:, h, 0:PARTS, t * P:(t + 1) * P], ps_turn[0][:], ACT.Copy
                                     ).then_inc(copied_a, 1)

            def high_part(b, g, s):
                act.wait_ge(qk_done, qk_step(b, g, s) + 1)
                nc.scalar.activation(hi[s % 2][:, s // 2 * BANK:(s // 2 + 1) * BANK], ps_side[:], ACT.Identity,
                                     bias=bias["qk"[s % 2]][:, g:g + 1]).then_inc(hi_done, 1)

            def copy_ht(b, s):
                act.wait_ge(ht_turned, b * HT_STEPS + (s + 1))
                c, k = s // DCH, s % DCH
                nc.scalar.activation(ht[:, k, c * BANK:(c + 1) * BANK], ps_side[:], ACT.Relu).then_inc(ht_done, 1)

            def copy_inv(b, g, u):
                act.wait_ge(inv_turned, unit(b, g, u) + (1 + START))
                act.wait_ge(heads_normed, unit(b, g, u) + START)
                nc.scalar.activation(inv_t[:], ps_side[:, 0:UNIT_Q], ACT.Copy).then_inc(inv_copied, 1)

            act.sem_inc(copied_a, START)
            act.wait_ge(weights_ready, 2)
            for s in range(HT_STEPS):
                copy_ht(0, s)
            for s in range(QK_STEPS):
                high_part(0, 0, s)
            exp(0, 0)

            def body(b, last):
                for g in range(PHASES):
                    for i in range(ROWS):
                        m = ahead(g, i, 1)
                        if not (last and m >= BATCH_ROWS):
                            exp(m, row(b, 0, m))
                        if i >= 1 and QK_SLOTS.get(i - 1, (0, 0))[1] == 1 and not (last and g == 1):
                            s = QK_SLOTS[i - 1][0]
                            if s == 0:
                                act.wait_ge(stacked[g], (b + 1) * (STACK_DMAS * 16))
                            high_part(*((b, 1) if g == 0 else (b + 1, 0)), s)
                        if g == 0 and i - 1 in HT_SLOTS and not last:
                            copy_ht(b + 1, HT_SLOTS[i - 1])
                        copy_a(b, g, i)
                        if i % UNIT_ROWS == UNIT_ROWS - 1:
                            copy_inv(b, g, i // UNIT_ROWS)

            batches(act, body)

        @block.vector
        def _(dve):
            def mask_row(m, n, qt):
                count = held(dve, n + 1)
                dve.wait_ge(mask_ready, 1)
                dve.wait_ge(scores_done, count)
                dve.wait_ge(turn_b, count)
                nc.vector.tensor_tensor_reduce(out=rows[:, m % RING, :], in0=ps_scores[m % 2][:],
                                               in1=mask[:, qt, :], scale=1.0, scalar=START_MIN,
                                               op0=ALU.add, op1=ALU.min,
                                               accum_out=row_min[:, m % RING:m % RING + 1]).then_inc(masked, 1)

            def tile_of(m):
                return m % ROWS // PARTS

            def copy_b(b, g, i):
                dve.wait_ge(turn_b, row(b, g, i) + (RING + 1))
                t, h = i // PARTS % UNIT_TILES, i % PARTS
                nc.vector.tensor_copy(turned_p[:, h, PARTS:TILES, t * P:(t + 1) * P], ps_turn[1][:]
                                      ).then_inc(copied_b, 1)

            def low_part(b, g, s):
                dve.wait_ge(hi_done, qk_step(b, g, s) + 1)
                cols = slice(s // 2 * BANK, (s // 2 + 1) * BANK)
                nc.vector.scalar_tensor_tensor(out=lo[s % 2][:, cols], in0=ps_side[:],
                                               scalar=bias["qk"[s % 2]][:, g:g + 1],
                                               in1=hi[s % 2][:, cols].bitcast(F32),
                                               op0=ALU.add, op1=ALU.subtract).then_inc(lo_done, 1)

            def copy_v(b, g, s):
                dve.wait_ge(v_done, v_step(b, g, s) + 1)
                nc.vector.tensor_tensor(v[g][:, s * PARTS:(s + 1) * PARTS, :],
                                        ps_side[:].rearrange("p (t n) -> p t n", n=P),
                                        bv_row[:, g * P:(g + 1) * P].unsqueeze(1).to_broadcast([P, PARTS, P]),
                                        ALU.add).then_inc(v_ready, 1)

            def moments(b, t):
                if t == 0:
                    dve.wait_ge(x_in, (b + 1) * 16)
                nc.vector.bn_stats(stats[:, t, :], xn[:, t, :]).then_inc(stats_done, 1)
                count = held(dve, b * TILES + (t + 1))
                dve.wait_ge(x_in, 16)
                dve.wait_ge(stats_done, count)
                nc.vector.bn_aggr(mean_var[:, t, :], stats[:, t, :]).then_inc(moments_done, 1)

            def invert(b, g, u):
                dve.wait_ge(exp_done, (unit(b, g, u) + 1) * UNIT_ROWS)
                dve.wait_ge(inv_spread, unit(b, g, u) + START)
                nc.vector.reciprocal(row_inv[:], row_sum[:, u % 2, :]).then_inc(inv_done, 1)

            def norm_heads(b, g, u):
                dve.wait_ge(inv_copied, unit(b, g, u) + 1)
                dve.wait_ge(heads_done, unit(b, g, u) + 1)
                dst = heads_t[0][:, u * UNIT_Q:(u + 1) * UNIT_Q] if g == 0 else heads_t[1][:, u % 2, :]
                nc.vector.tensor_tensor(dst, ps_heads[:, 0:UNIT_Q], inv_t[:], ALU.mult
                                        ).then_inc(heads_normed, 1)

            def finish(b, u):
                dve.wait_ge(o_done, b * UNITS + (u + 1))
                dve.wait_ge(res_ready, b * UNITS + (u + 1))
                nc.vector.tensor_tensor(res[:, u % 2], ps_side[:].rearrange("p (t d) -> p t d", d=DIM),
                                        res[:, u % 2], ALU.add).then_inc(out_ready, 1)

            dve.sem_inc(copied_b, START)
            dve.sem_inc(heads_normed, START)
            for t in range(TILES):
                moments(0, t)
            dve.wait_ge(weights_in, 8 * 16)
            nc.vector.tensor_scalar(w["q"][:], w["q"][:], -SCALE, None, ALU.mult).then_inc(weights_ready, 1)
            nc.vector.tensor_scalar(bias["q"][:], bias["q"][:], -SCALE, None, ALU.mult).then_inc(weights_ready, 1)
            dve.wait_ge(weights_ready, 2)
            for s in range(QK_STEPS):
                low_part(0, 0, s)
            dve.wait_ge(mask_in, 16)
            nc.vector.tensor_scalar(mask[:], mask[:], 1.0, -MASKED, ALU.subtract, ALU.mult).then_inc(mask_ready, 1)
            dve.wait_ge(mask_ready, 1)
            for s in range(V_STEPS):
                copy_v(0, 0, s)
            mask_row(0, 0, 0)
            mask_row(1, 1, 0)

            def body(b, last):
                for g in range(PHASES):
                    for i in range(ROWS):
                        m = ahead(g, i, 2)
                        if not (last and m >= BATCH_ROWS):
                            mask_row(m, row(b, 0, m), tile_of(m))
                        if i >= 1 and QK_SLOTS.get(i - 1, (0, 0))[1] == 1 and not (last and g == 1):
                            low_part(*((b, 1) if g == 0 else (b + 1, 0)), QK_SLOTS[i - 1][0])
                        if V_SLOTS[g].get(i - 1, (0, 0))[1] == 1 and not (last and g == 1):
                            copy_v(*((b, 1) if g == 0 else (b + 1, 0)), V_SLOTS[g][i - 1][0])
                        if g == 1 and O_SLOTS.get(i - 1, (0, 0))[1] == 1:
                            finish(b, O_SLOTS[i - 1][0])
                        if g == 0 and STATS_SLOT <= i < STATS_SLOT + TILES and not last:
                            moments(b + 1, i - STATS_SLOT)
                        copy_b(b, g, i)
                        if i % UNIT_ROWS == UNIT_ROWS - 2:
                            invert(b, g, i // UNIT_ROWS)
                        if i % UNIT_ROWS == NORM_ROW:
                            if i > UNIT_ROWS:
                                norm_heads(b, g, i // UNIT_ROWS - 1)
                            elif g == 1:
                                norm_heads(b, 0, UNITS - 1)
                norm_heads(b, 1, UNITS - 1)
                finish(b, UNITS - 1)

            batches(dve, body)

        @block.tensor
        def _(pe):
            def side_wait(b, what, g, s, last):
                names = [o for o in order if not (last and (o[0] == "ht" or (o[1] == 1 and o[0] in ("qk", "v"))))]
                k = names.index((what, g, s))
                if k == 0:
                    pe.wait_ge(v_ready, v_step(b, 0, V_STEPS - 1) + 1)
                    return
                kind, pg, ps = names[k - 1]
                nb, ng = (b, 1) if pg == 0 else (b + 1, 0)
                if kind == "qk":
                    pe.wait_ge(lo_done, qk_step(nb, ng, ps) + 1)
                elif kind == "v":
                    pe.wait_ge(v_ready, v_step(nb, ng, ps) + 1)
                elif kind == "ht":
                    pe.wait_ge(ht_done, (b + 1) * HT_STEPS + (ps + 1))
                elif kind == "inv":
                    pe.wait_ge(inv_copied, unit(b, pg, ps) + 1)
                else:
                    pe.wait_ge(out_ready, b * UNITS + (ps + 1))

            def scores(m, n, wait_free=True):
                g, i = m // ROWS % PHASES, m % ROWS
                qt, h = i // PARTS, i % PARTS
                if wait_free:
                    pe.wait_ge(masked, n - 1)
                for c in range(CHUNKS):
                    mm = nc.tensor.matmul(ps_scores[m % 2][:, c * BANK:(c + 1) * BANK],
                                          q_stack[g][:, h, qt * P:(qt + 1) * P],
                                          k_stack[g][:, h, c * BANK:(c + 1) * BANK], start=True, stop=True)
                mm.then_inc(scores_done, 1)

            def turn(b, g, i):
                n = row(b, g, i)
                pe.wait_ge(exp_done, n + 1)
                for half, (bank, done, copied) in enumerate(((ps_turn[0], turn_a, copied_a),
                                                            (ps_turn[1], turn_b, copied_b))):
                    pe.wait_ge(copied, n + START)
                    for k in range(PARTS):
                        kt = half * PARTS + k
                        tr = nc.tensor.transpose(bank[:, k, :], rows[:, i % RING, kt * P:(kt + 1) * P], ident[:])
                    tr.then_inc(done, 1)

            def qk(b, g, s, k):
                n = "qk"[s % 2]
                mm = nc.tensor.matmul(ps_side[:], w[n][:, k, g * P:(g + 1) * P],
                                      ht[:, k, s // 2 * BANK:(s // 2 + 1) * BANK],
                                      start=(k == 0), stop=(k == DCH - 1))
                if k == DCH - 1:
                    mm.then_inc(qk_done, 1)

            def values(g, s, half):
                for t in range(half * 2, half * 2 + 2):
                    tok = slice((s * PARTS + t) * P, (s * PARTS + t + 1) * P)
                    for k in range(DCH):
                        mm = nc.tensor.matmul(ps_side[:, t * P:(t + 1) * P], ht[:, k, tok],
                                              w["v"][:, k, g * P:(g + 1) * P], start=(k == 0), stop=(k == DCH - 1))
                if half == 1:
                    mm.then_inc(v_done, 1)

            def turn_ht(s):
                c, k = s // DCH, s % DCH
                for t in range(PARTS):
                    tr = nc.tensor.transpose(ps_side[:, t * P:(t + 1) * P],
                                             xn[:, c * PARTS + t, k * P:(k + 1) * P], ident[:])
                tr.then_inc(ht_turned, 1)

            def project_out(u, half):
                t = half
                q0 = u * UNIT_Q + t * P
                lhs = (heads_t[0][:, q0:q0 + P], heads_t[1][:, u % 2, t * P:(t + 1) * P])
                for g in range(PHASES):
                    mm = nc.tensor.matmul(ps_side[:, t * DIM:(t + 1) * DIM], lhs[g], w["o"][:, g, :],
                                          start=(g == 0), stop=(g == PHASES - 1))
                if half == 1:
                    mm.then_inc(o_done, 1)

            def turn_inv():
                for t in range(UNIT_TILES):
                    tr = nc.tensor.transpose(ps_side[:, t * P:(t + 1) * P],
                                             inv_wide[:, t].rearrange("p h d -> p (h d)"), ident[:])
                tr.then_inc(inv_turned, 1)

            def heads(g):
                for kt in range(TILES):
                    for h in range(PARTS):
                        mm = nc.tensor.matmul(ps_heads[h * HEAD_DIM:(h + 1) * HEAD_DIM, 0:UNIT_Q],
                                              v[g][:, kt, h * HEAD_DIM:(h + 1) * HEAD_DIM],
                                              turned_p[:, h, kt, :], start=(kt == 0), stop=(kt == TILES - 1))
                mm.then_inc(heads_done, 1)

            pe.sem_inc(inv_turned, START)
            pe.wait_ge(ident_ready, 1)
            pe.wait_ge(normed, TILES)
            for s in range(HT_STEPS):
                if s:
                    pe.wait_ge(ht_done, s)
                turn_ht(s)
            pe.wait_ge(weights_ready, 2)
            pe.wait_ge(ht_done, HT_STEPS)
            for s in range(QK_STEPS):
                if s:
                    pe.wait_ge(lo_done, s)
                for k in range(DCH):
                    qk(0, 0, s, k)
            pe.wait_ge(lo_done, QK_STEPS)
            for s in range(V_STEPS):
                if s:
                    pe.wait_ge(v_ready, s)
                values(0, s, 0)
                values(0, s, 1)
            pe.wait_ge(stacked[0], STACK_DMAS * 16)
            scores(0, 0, False)
            scores(1, 1, False)
            scores(2, 2)

            def body(b, last):
                for g in range(PHASES):
                    for i in range(ROWS):
                        turn(b, g, i)
                        m = ahead(g, i, 3)
                        if not (last and m >= BATCH_ROWS):
                            if m % ROWS == 0:
                                pe.wait_ge(stacked[1 - g], (b + (1 + g)) * (STACK_DMAS * 16))
                            scores(m, row(b, 0, m))
                        prepare = not (last and g == 1)
                        ng = 1 - g
                        if i in QK_SLOTS and prepare:
                            s, k = QK_SLOTS[i]
                            if k == 0:
                                side_wait(b, "qk", g, s, last)
                            qk(b, ng, s, k)
                        if i in V_SLOTS[g] and prepare:
                            s, half = V_SLOTS[g][i]
                            if half == 0:
                                side_wait(b, "v", g, s, last)
                            values(ng, s, half)
                        if g == 0 and i in HT_SLOTS and not last:
                            s = HT_SLOTS[i]
                            side_wait(b, "ht", g, s, last)
                            if s == 0:
                                pe.wait_ge(normed, (b + 2) * TILES)
                            turn_ht(s)
                        if g == 1 and i in O_SLOTS:
                            u, half = O_SLOTS[i]
                            if half == 0:
                                side_wait(b, "o", g, u, last)
                                pe.wait_ge(heads_normed, unit(b, 1, u) + (1 + START))
                            project_out(u, half)
                        if i % UNIT_ROWS == UNIT_ROWS - 1:
                            u = i // UNIT_ROWS
                            side_wait(b, "inv", g, u, last)
                            pe.wait_ge(inv_spread, unit(b, g, u) + (1 + START))
                            turn_inv()
                            pe.wait_ge(copied_a, row(b, g, i) + (1 + START))
                            pe.wait_ge(copied_b, row(b, g, i) + (1 + START))
                            pe.wait_ge(heads_normed, unit(b, g, u) + START)
                            heads(g)
                side_wait(b, "o", 1, UNITS - 1, last)
                pe.wait_ge(heads_normed, unit(b, 1, UNITS - 1) + (1 + START))
                project_out(UNITS - 1, 0)
                project_out(UNITS - 1, 1)
                if not last:
                    pe.wait_ge(out_ready, b * UNITS + UNITS)

            batches(pe, body)


_INS = ["x", "adj", "L0_gnn_Wq", "L0_gnn_bq", "L0_gnn_Wk", "L0_gnn_bk", "L0_gnn_Wv", "L0_gnn_bv",
        "L0_gnn_Wo", "L0_gnn_bo"]


def kernel(**inputs):
    import numpy as _np
    import concourse.bacc as _bacc
    from concourse.bass_utils import run_bass_kernel_spmd as _run

    nc = _bacc.Bacc("TRN2", target_bir_lowering=False, num_devices=1)
    arrays, args = {}, []
    for name in _INS:
        a = _np.ascontiguousarray(inputs[name])
        arrays[f"in_{name}"] = a
        args.append(nc.dram_tensor(f"in_{name}", a.shape, mybir.dt.from_np(a.dtype), kind="ExternalInput").ap())
    args.append(nc.dram_tensor("out_0", (BATCH, TOKENS, DIM), F32, kind="ExternalOutput").ap())
    gnn_kernel(nc, *args)
    r = _run(nc, [arrays], core_ids=[0])
    return r.results[0]["out_0"]
```

```python
from contextlib import ExitStack

import concourse.bass as bass
from concourse import mybir

F32 = mybir.dt.float32
F32R = mybir.dt.float32r
ALU = mybir.AluOpType
ACT = mybir.ActivationFunctionType

P = 128
BANK = 512
BATCH, TOKENS, DIM, HEADS = 8, 1024, 256, 8
HEAD_DIM = DIM // HEADS
PARTS = P // HEAD_DIM
PHASES = HEADS // PARTS
TILES = TOKENS // P
DCH = DIM // P
CHUNKS = TOKENS // BANK
UNIT_TILES = 2
UNIT_Q = UNIT_TILES * P
UNIT_ROWS = UNIT_TILES * PARTS
UNITS = TILES // UNIT_TILES
ROWS = UNITS * UNIT_ROWS
BATCH_ROWS = PHASES * ROWS
BATCH_UNITS = PHASES * UNITS
RING = 4

EPS = 1e-5
MASKED = 1e9
START_MIN = 3.0e38

QK_STEPS = 2 * CHUNKS
V_STEPS = TILES * P // BANK
HT_STEPS = DCH * CHUNKS
PREP_STEPS = HT_STEPS + QK_STEPS + V_STEPS
HEAD_DMAS = 2 * PARTS

SIDE = ({1: ("inv", 0, 0, 1), 3: ("o", 3, 0, 2), 4: ("o", 3, 1, 2), 5: ("qk", 0, 0, 2), 6: ("qk", 0, 1, 2),
         9: ("inv", 0, 0, 1), 10: ("qk", 1, 0, 2), 11: ("qk", 1, 1, 2), 12: ("qk", 2, 0, 2), 13: ("qk", 2, 1, 2),
         14: ("qk", 3, 0, 2), 15: ("qk", 3, 1, 2), 17: ("inv", 0, 0, 1), 18: ("v", 0, 0, 2), 19: ("v", 0, 1, 2),
         20: ("v", 1, 0, 2), 21: ("v", 1, 1, 2), 22: ("ht", 0, 0, 1), 23: ("ht", 1, 0, 1), 25: ("inv", 0, 0, 1),
         26: ("ht", 2, 0, 1), 27: ("ht", 3, 0, 1)},
        {1: ("inv", 0, 0, 1), 2: ("qk", 0, 0, 2), 3: ("qk", 0, 1, 2), 4: ("qk", 1, 0, 2), 5: ("qk", 1, 1, 2),
         6: ("qk", 2, 0, 2), 7: ("qk", 2, 1, 2), 9: ("inv", 0, 0, 1), 10: ("qk", 3, 0, 2), 11: ("qk", 3, 1, 2),
         12: ("o", 0, 0, 2), 13: ("o", 0, 1, 2), 14: ("v", 0, 0, 2), 15: ("v", 0, 1, 2), 17: ("inv", 0, 0, 1),
         18: ("v", 1, 0, 2), 19: ("v", 1, 1, 2), 20: ("o", 1, 0, 2), 21: ("o", 1, 1, 2), 25: ("inv", 0, 0, 1),
         28: ("o", 2, 0, 2), 29: ("o", 2, 1, 2)})
HEAD = 7
NORM_ROW = 2
STATS_SLOT = 8


def side_work(g, i, first, last):
    work = SIDE[g].get(i)
    if work is None:
        return None
    kind = work[0]
    if first and g == 0 and i < HEAD and kind in ("inv", "o"):
        return None
    if last and (kind == "ht" or g == 1 and kind in ("qk", "v")):
        return None
    return work



def gnn_kernel(nc, x, adj, Wq, bq, Wk, bk, Wv, bv, Wo, bo, out):
    SCALE = float(HEAD_DIM) ** -0.5
    x_v = x.rearrange("b (t p) d -> b p t d", p=P)
    out_v = out.rearrange("b (t p) d -> b p t d", p=P)
    adj_v = adj.rearrange("(t p) k -> p t k", p=P)

    with ExitStack() as ctx:
        def sb(name, shape, dt=F32):
            return ctx.enter_context(nc.sbuf_tensor(name, shape, dt))

        def pb(name, shape, dt=F32):
            return ctx.enter_context(nc.psum_tensor(name, shape, dt))

        def sem(name):
            return ctx.enter_context(nc.semaphore(name))

        mask = sb("mask", [P, TILES, TOKENS])
        q_stack = [sb(f"q_stack{g}", [P, PARTS, TOKENS], F32R) for g in range(PHASES)]
        k_stack = [sb(f"k_stack{g}", [P, PARTS, TOKENS], F32R) for g in range(PHASES)]
        rows = sb("rows", [P, RING, TOKENS])
        turned_p = sb("turned_p", [P, PARTS, TILES, UNIT_Q])
        hi = [sb(f"{n}_hi", [P, TOKENS], F32R) for n in "qk"]
        lo = [sb(f"{n}_lo", [P, TOKENS], F32R) for n in "qk"]
        ht = sb("ht", [P, DCH, TOKENS])
        xn = sb("xn", [P, TILES, DIM])
        v = [sb(f"v{g}", [P, TILES, P]) for g in range(PHASES)]
        w = {n: sb(f"w{n}", [P, DCH, DIM]) for n in "qkvo"}
        heads_t = [sb("heads_t0", [P, TOKENS]), sb("heads_t1", [P, 2, UNIT_Q])]
        res = sb("res", [P, 2, UNIT_TILES, DIM])
        inv_wide = sb("inv_wide", [P, UNIT_TILES, PARTS, HEAD_DIM])
        inv_t = sb("inv_t", [P, UNIT_Q])
        ident = sb("ident", [P, P])
        bv_row = sb("bv_row", [P, DIM])
        bo_row = sb("bo_row", [P, DIM])
        bias = {n: sb(f"b{n}_col", [P, PHASES]) for n in "qk"}
        row_min = sb("row_min", [P, RING])
        row_sum = sb("row_sum", [P, 2, UNIT_ROWS])
        row_inv = sb("row_inv", [P, UNIT_ROWS])
        stats = sb("stats", [P, TILES, 6])
        mean_var = sb("mean_var", [P, TILES, 2])
        ln = {n: sb(f"ln_{n}", [P, TILES]) for n in ("neg_mean", "var", "power", "rstd", "t0", "t1", "t2")}

        ps_scores = [pb(f"ps_scores{i}", [P, TOKENS]) for i in range(2)]
        ps_turn = [pb(f"ps_turn{i}", [P, PARTS, P]) for i in range(2)]
        ps_heads = pb("ps_heads", [P, BANK])
        ps_side = pb("ps_side", [P, BANK])

        START = 1
        weights_in = sem("weights_in")
        mask_in = sem("mask_in")
        x_in = sem("x_in")
        res_in = [sem(f"res_in{i}") for i in range(2)]
        stacked = [[sem(f"stacked{g}_{h}") for h in range(PARTS)] for g in range(PHASES)]
        out_stored = sem("out_stored")
        weights_ready = sem("weights_ready")
        mask_ready = sem("mask_ready")
        ident_ready = sem("ident_ready")
        stats_done = sem("stats_done")
        moments_done = sem("moments_done")
        ln_chain = sem("ln_chain")
        normed = sem("normed")
        scores_done = sem("scores_done")
        masked = sem("masked")
        exp_done = sem("exp_done")
        turn_a = sem("turn_a")
        turn_b = sem("turn_b")
        copied_a = sem("copied_a")
        copied_b = sem("copied_b")
        heads_done = sem("heads_done")
        inv_done = sem("inv_done")
        inv_spread = sem("inv_spread")
        inv_turned = sem("inv_turned")
        inv_copied = sem("inv_copied")
        heads_normed = sem("heads_normed")
        ht_turned = sem("ht_turned")
        ht_done = sem("ht_done")
        qk_done = sem("qk_done")
        hi_done = sem("hi_done")
        lo_done = sem("lo_done")
        v_done = sem("v_done")
        v_ready = sem("v_ready")
        o_done = sem("o_done")
        res_ready = sem("res_ready")
        out_ready = sem("out_ready")

        def row(b, g, i):
            return b * BATCH_ROWS + (g * ROWS + i)

        def unit(b, g, u):
            return b * BATCH_UNITS + (g * UNITS + u)

        def ahead(g, i, k):
            return g * ROWS + i + k

        def qk_step(b, g, s):
            return b * (2 * QK_STEPS) + (g * QK_STEPS + s)

        def v_step(b, g, s):
            return b * (2 * V_STEPS) + (g * V_STEPS + s)

        def held(eng, count):
            return count if isinstance(count, int) else eng.snap(eng.to_reg(count))

        def slots(eng, slot, tail):
            def rest_of(b, last):
                for g in range(PHASES):
                    for i in range(HEAD if g == 0 else 0, ROWS):
                        slot(b, g, i, False, last)

            for i in range(HEAD):
                slot(0, 0, i, True, False)
            with eng.Fori(0, BATCH - 1) as b:
                rest_of(b, False)
                for i in range(HEAD):
                    slot(b + 1, 0, i, False, False)
            rest_of(BATCH - 1, True)
            tail()

        block = ctx.enter_context(nc.Block())

        @block.sync
        def _(sp):
            def load_x(b):
                sp.dma_start(xn[:], x_v[b]).then_inc(x_in, 16)

            def load_res(b, u):
                sp.dma_start(res[:, u % 2], x_v[b, :, u * UNIT_TILES:(u + 1) * UNIT_TILES, :]
                             ).then_inc(res_in[u % 2], 16)

            def stack(bg, g, rows_before):
                if rows_before is not None:
                    sp.wait_ge(scores_done, rows_before)
                sp.wait_ge(lo_done, qk_step(bg, g, QK_STEPS - 1) + 1)
                for h in range(PARTS):
                    for dst, parts in ((q_stack[g], (hi[0], lo[0], hi[0], lo[0])),
                                       (k_stack[g], (hi[1], hi[1], lo[1], lo[1]))):
                        for r in range(PARTS):
                            sp.dma_start(dst[r * HEAD_DIM:(r + 1) * HEAD_DIM, h, :].bitcast(F32),
                                         parts[r][h * HEAD_DIM:(h + 1) * HEAD_DIM, :].bitcast(F32)
                                         ).then_inc(stacked[g][h], 16)

            load_x(0)
            for n, src in zip("qkvo", (Wq, Wk, Wv, Wo)):
                sp.dma_start(w[n][:], src.rearrange("(c p) n -> p c n", p=P)).then_inc(weights_in, 16)
            for n, src in zip("qk", (bq, bk)):
                sp.dma_start(bias[n][:], src.rearrange("(g p) -> p g", p=P), allow_slow_non_contiguous=True).then_inc(weights_in, 16)
            for row_t, src in ((bv_row, bv), (bo_row, bo)):
                sp.dma_start(row_t[:], src.partition_broadcast(P)).then_inc(weights_in, 16)
            sp.dma_start(mask[:], adj_v).then_inc(mask_in, 16)
            load_res(0, 0)
            load_res(0, 1)
            stack(0, 0, None)

            sp.wait_ge(ht_turned, HT_STEPS)
            load_x(1)

            def body(b, left):
                stack(b, 1, row(b, 0, 0) + 1)
                if left > 1:
                    sp.wait_ge(ht_turned, b * HT_STEPS + 2 * HT_STEPS)
                    load_x(b + 2)
                if left > 0:
                    stack(b + 1, 0, row(b, 1, 0))
                for u in range(UNITS):
                    sp.wait_ge(out_ready, b * UNITS + (u + 1))
                    sp.dma_start(out_v[b, :, u * UNIT_TILES:(u + 1) * UNIT_TILES, :], res[:, u % 2]
                                 ).then_inc(out_stored, 16)
                    if u + 2 < UNITS or left > 0:
                        sp.wait_ge(out_stored, (b * UNITS + (u + 1)) * 16)
                        load_res(*((b, u + 2) if u + 2 < UNITS else (b + 1, u + 2 - UNITS)))

            with sp.Fori(0, BATCH - 2) as b:
                body(b, 2)
            body(BATCH - 2, 1)
            body(BATCH - 1, 0)
            sp.wait_ge(out_stored, BATCH * UNITS * 16)

        @block.gpsimd
        def _(pool):
            pool.sem_inc(inv_spread, START)
            pool.memset(ident[:], 0.0).then_inc(turn_b, RING)
            pool.wait_ge(turn_b, RING)
            pool.affine_select(out=ident[:], in_=ident[:], compare_op=ALU.not_equal, fill=1.0, base=0,
                               pattern=[[-1, P]], channel_multiplier=1).then_inc(ident_ready, 1)
            pool.memset(ln["power"][:], -0.5).then_inc(ln_chain, 1)
            pool.wait_ge(weights_in, 8 * 16)

            LN_STEPS = 7

            def own():
                pool.wait_ge(ident_ready, 1)

            def norm(b):
                base = b * LN_STEPS + 1
                count = held(pool, b * TILES + TILES)
                own()
                pool.wait_ge(moments_done, count)
                mean, var = mean_var[:, :, 0], mean_var[:, :, 1]
                pool.tensor_scalar(ln["neg_mean"][:], mean, -1.0, None, ALU.mult).then_inc(ln_chain, 1)
                pool.tensor_scalar(ln["var"][:], var, EPS, None, ALU.add).then_inc(ln_chain, 1)
                pool.wait_ge(ln_chain, base + 2)
                pool.tensor_tensor(ln["t0"][:], ln["var"][:], ln["power"][:], ALU.pow).then_inc(ln_chain, 1)
                pool.wait_ge(ln_chain, base + 3)
                pool.tensor_tensor(ln["t1"][:], ln["t0"][:], ln["t0"][:], ALU.mult).then_inc(ln_chain, 1)
                pool.wait_ge(ln_chain, base + 4)
                pool.tensor_tensor(ln["t2"][:], ln["t1"][:], ln["var"][:], ALU.mult).then_inc(ln_chain, 1)
                count = held(pool, base + 5)
                own()
                pool.wait_ge(ln_chain, count)
                pool.tensor_scalar(ln["t1"][:], ln["t2"][:], -0.5, 1.5, ALU.mult, ALU.add).then_inc(ln_chain, 1)
                pool.wait_ge(ln_chain, base + 6)
                pool.tensor_tensor(ln["rstd"][:], ln["t0"][:], ln["t1"][:], ALU.mult).then_inc(ln_chain, 1)
                count = held(pool, base + 7)
                own()
                pool.wait_ge(ln_chain, count)
                for t in range(TILES):
                    pool.tensor_scalar(xn[:, t, :], xn[:, t, :], ln["neg_mean"][:, t:t + 1],
                                       ln["rstd"][:, t:t + 1], ALU.add, ALU.mult).then_inc(normed, 1)

            norm(0)

            def body(b, last):
                for g in range(PHASES):
                    for u in range(UNITS):
                        count = held(pool, unit(b, g, u) + 1)
                        own()
                        pool.wait_ge(inv_done, count)
                        pool.wait_ge(inv_turned, count)
                        pool.tensor_copy(inv_wide[:], row_inv[:].rearrange("p (t h) -> p t h", h=PARTS)
                                         .unsqueeze(3).to_broadcast([P, UNIT_TILES, PARTS, HEAD_DIM])
                                         ).then_inc(inv_spread, 1)
                        if g == 0 and u == 1 and not last:
                            norm(b + 1)
                        if g == 0 and u == 3 or g == 1 and u < UNITS - 1:
                            k = 0 if g == 0 else u + 1
                            pool.wait_ge(res_in[k % 2], (b * (UNITS // 2) + (k // 2 + 1)) * 16)
                            pool.tensor_tensor(res[:, k % 2], res[:, k % 2],
                                               bo_row[:].unsqueeze(1).to_broadcast([P, UNIT_TILES, DIM]),
                                               ALU.add).then_inc(res_ready, 1)

            with pool.Fori(0, BATCH - 1) as b:
                body(b, False)
            body(BATCH - 1, True)

        @block.scalar
        def _(act):
            def exp(m, n):
                act.wait_ge(masked, n + 1)
                u, j = m // UNIT_ROWS, m % UNIT_ROWS
                nc.scalar.activation(rows[:, m % RING, :], rows[:, m % RING, :], ACT.Exp,
                                     bias=row_min[:, m % RING:m % RING + 1], scale=-1.0,
                                     accum_out=row_sum[:, u % 2, j:j + 1]).then_inc(exp_done, 1)

            def copy_a(b, g, i):
                act.wait_ge(turn_a, row(b, g, i) + 1)
                t, h = i // PARTS % UNIT_TILES, i % PARTS
                nc.scalar.activation(turned_p[:, h, 0:PARTS, t * P:(t + 1) * P], ps_turn[0][:], ACT.Copy
                                     ).then_inc(copied_a, 1)

            def high_part(b, g, s):
                act.wait_ge(qk_done, qk_step(b, g, s) + 1)
                nc.scalar.activation(hi[s % 2][:, s // 2 * BANK:(s // 2 + 1) * BANK], ps_side[:], ACT.Identity,
                                     bias=bias["qk"[s % 2]][:, g:g + 1]).then_inc(hi_done, 1)

            def copy_ht(b, s):
                act.wait_ge(ht_turned, b * HT_STEPS + (s + 1))
                c, k = s // DCH, s % DCH
                nc.scalar.activation(ht[:, k, c * BANK:(c + 1) * BANK], ps_side[:], ACT.Relu).then_inc(ht_done, 1)

            def copy_inv(turned):
                act.wait_ge(inv_turned, turned + START)
                act.wait_ge(heads_normed, turned - 1 + START)
                nc.scalar.activation(inv_t[:], ps_side[:, 0:UNIT_Q], ACT.Copy).then_inc(inv_copied, 1)

            act.sem_inc(copied_a, START)
            act.wait_ge(weights_ready, 2)
            for s in range(HT_STEPS):
                copy_ht(0, s)
            for s in range(QK_STEPS):
                high_part(0, 0, s)
            exp(0, 0)

            def slot(b, g, i, first, last):
                m = ahead(g, i, 1)
                if not (last and m >= BATCH_ROWS):
                    exp(m, row(b, 0, m))
                kind, s, part, parts = side_work(g, i - 1, first, last) or (None, 0, 0, 0)
                if kind == "inv":
                    copy_inv(unit(b, g, i // UNIT_ROWS))
                if kind == "ht":
                    copy_ht(b + 1, s)
                if kind == "qk" and part == parts - 1:
                    if s == 0:
                        for h in range(PARTS):
                            act.wait_ge(stacked[g][h], (b + 1) * (HEAD_DMAS * 16))
                    high_part(*((b, 1) if g == 0 else (b + 1, 0)), s)
                copy_a(b, g, i)

            def tail():
                copy_inv(BATCH * BATCH_UNITS)

            slots(act, slot, tail)

        @block.vector
        def _(dve):
            def mask_row(m, n, qt):
                count = held(dve, n + 1)
                dve.wait_ge(mask_ready, 1)
                dve.wait_ge(scores_done, count)
                dve.wait_ge(turn_b, count)
                nc.vector.tensor_tensor_reduce(out=rows[:, m % RING, :], in0=ps_scores[m % 2][:],
                                               in1=mask[:, qt, :], scale=1.0, scalar=START_MIN,
                                               op0=ALU.add, op1=ALU.min,
                                               accum_out=row_min[:, m % RING:m % RING + 1]).then_inc(masked, 1)

            def tile_of(m):
                return m % ROWS // PARTS

            def copy_b(b, g, i):
                dve.wait_ge(turn_b, row(b, g, i) + (RING + 1))
                t, h = i // PARTS % UNIT_TILES, i % PARTS
                nc.vector.tensor_copy(turned_p[:, h, PARTS:TILES, t * P:(t + 1) * P], ps_turn[1][:]
                                      ).then_inc(copied_b, 1)

            def low_part(b, g, s):
                dve.wait_ge(hi_done, qk_step(b, g, s) + 1)
                cols = slice(s // 2 * BANK, (s // 2 + 1) * BANK)
                nc.vector.scalar_tensor_tensor(out=lo[s % 2][:, cols], in0=ps_side[:],
                                               scalar=bias["qk"[s % 2]][:, g:g + 1],
                                               in1=hi[s % 2][:, cols].bitcast(F32),
                                               op0=ALU.add, op1=ALU.subtract).then_inc(lo_done, 1)

            def copy_v(b, g, s):
                dve.wait_ge(v_done, v_step(b, g, s) + 1)
                nc.vector.tensor_tensor(v[g][:, s * PARTS:(s + 1) * PARTS, :],
                                        ps_side[:].rearrange("p (t n) -> p t n", n=P),
                                        bv_row[:, g * P:(g + 1) * P].unsqueeze(1).to_broadcast([P, PARTS, P]),
                                        ALU.add).then_inc(v_ready, 1)

            def moments(b, t):
                if t == 0:
                    dve.wait_ge(x_in, (b + 1) * 16)
                nc.vector.bn_stats(stats[:, t, :], xn[:, t, :]).then_inc(stats_done, 1)
                count = held(dve, b * TILES + (t + 1))
                dve.wait_ge(x_in, 16)
                dve.wait_ge(stats_done, count)
                nc.vector.bn_aggr(mean_var[:, t, :], stats[:, t, :]).then_inc(moments_done, 1)

            def invert(before, u):
                dve.wait_ge(exp_done, before * UNIT_ROWS)
                dve.wait_ge(inv_spread, before - 1 + START)
                nc.vector.reciprocal(row_inv[:], row_sum[:, u % 2, :]).then_inc(inv_done, 1)

            def norm_heads(before, g, u):
                dve.wait_ge(inv_copied, before)
                dve.wait_ge(heads_done, before)
                dst = heads_t[0][:, u * UNIT_Q:(u + 1) * UNIT_Q] if g == 0 else heads_t[1][:, u % 2, :]
                nc.vector.tensor_tensor(dst, ps_heads[:, 0:UNIT_Q], inv_t[:], ALU.mult
                                        ).then_inc(heads_normed, 1)

            def finish(count, u):
                dve.wait_ge(o_done, count)
                dve.wait_ge(res_ready, count)
                nc.vector.tensor_tensor(res[:, u % 2], ps_side[:].rearrange("p (t d) -> p t d", d=DIM),
                                        res[:, u % 2], ALU.add).then_inc(out_ready, 1)

            dve.sem_inc(copied_b, START)
            dve.sem_inc(heads_normed, START)
            for t in range(TILES):
                moments(0, t)
            dve.wait_ge(weights_in, 8 * 16)
            nc.vector.tensor_scalar(w["q"][:], w["q"][:], -SCALE, None, ALU.mult).then_inc(weights_ready, 1)
            nc.vector.tensor_scalar(bias["q"][:], bias["q"][:], -SCALE, None, ALU.mult).then_inc(weights_ready, 1)
            dve.wait_ge(weights_ready, 2)
            for s in range(QK_STEPS):
                low_part(0, 0, s)
            dve.wait_ge(mask_in, 16)
            nc.vector.tensor_scalar(mask[:], mask[:], 1.0, -MASKED, ALU.subtract, ALU.mult).then_inc(mask_ready, 1)
            dve.wait_ge(mask_ready, 1)
            for s in range(V_STEPS):
                copy_v(0, 0, s)
            mask_row(0, 0, 0)
            mask_row(1, 1, 0)

            def slot(b, g, i, first, last):
                m = ahead(g, i, 2)
                if not (last and m >= BATCH_ROWS):
                    mask_row(m, row(b, 0, m), tile_of(m))
                kind, s, part, parts = side_work(g, i - 1, first, last) or (None, 0, 0, 0)
                if kind in ("qk", "v") and part == parts - 1:
                    {"qk": low_part, "v": copy_v}[kind](*((b, 1) if g == 0 else (b + 1, 0)), s)
                if kind == "o" and part == parts - 1:
                    finish(b * UNITS + (0 if g == 0 else s + 1), s)
                if g == 0 and STATS_SLOT <= i < STATS_SLOT + TILES and not last:
                    moments(b + 1, i - STATS_SLOT)
                u = i // UNIT_ROWS
                if not (first and i < HEAD):
                    pg, pu = (g, u - 1) if u else (1 - g, UNITS - 1)
                    if i % UNIT_ROWS == 0:
                        invert(unit(b, g, u), pu)
                    if i % UNIT_ROWS == NORM_ROW:
                        norm_heads(unit(b, g, u), pg, pu)
                copy_b(b, g, i)

            def tail():
                units = BATCH * BATCH_UNITS
                invert(units, UNITS - 1)
                norm_heads(units, 1, UNITS - 1)
                finish(BATCH * UNITS, UNITS - 1)

            slots(dve, slot, tail)

        @block.tensor
        def _(pe):
            def side_wait(b, g, i, first, last):
                pg, pi = g, i - 1
                while pi >= 0 or pg == 1:
                    if pi < 0:
                        pg, pi = 0, ROWS - 1
                    if side_work(pg, pi, first, last) is not None:
                        break
                    pi -= 1
                if pi < 0:
                    if first:
                        pe.wait_ge(v_ready, V_STEPS)
                    else:
                        pe.wait_ge(out_ready, b * UNITS - 1)
                    return
                kind, s, _, _ = side_work(pg, pi, first, last)
                nb, ng = (b, 1) if pg == 0 else (b + 1, 0)
                if kind == "qk":
                    pe.wait_ge(lo_done, qk_step(nb, ng, s) + 1)
                elif kind == "v":
                    pe.wait_ge(v_ready, v_step(nb, ng, s) + 1)
                elif kind == "ht":
                    pe.wait_ge(ht_done, (b + 1) * HT_STEPS + (s + 1))
                elif kind == "inv":
                    pe.wait_ge(inv_copied, unit(b, pg, pi // UNIT_ROWS))
                else:
                    pe.wait_ge(out_ready, b * UNITS + (0 if pg == 0 else s + 1))

            def scores(m, n, wait_free, fills):
                g, i = m // ROWS % PHASES, m % ROWS
                qt, h = i // PARTS, i % PARTS
                if fills is not None:
                    pe.wait_ge(stacked[g][h], fills * (HEAD_DMAS * 16))
                if wait_free:
                    pe.wait_ge(masked, n - 1)
                for c in range(CHUNKS):
                    mm = nc.tensor.matmul(ps_scores[m % 2][:, c * BANK:(c + 1) * BANK],
                                          q_stack[g][:, h, qt * P:(qt + 1) * P],
                                          k_stack[g][:, h, c * BANK:(c + 1) * BANK], start=True, stop=True)
                mm.then_inc(scores_done, 1)

            def turn(b, g, i, half):
                n = row(b, g, i)
                bank, done, copied = ((ps_turn[0], turn_a, copied_a), (ps_turn[1], turn_b, copied_b))[half]
                if half == 0:
                    pe.wait_ge(exp_done, n + 1)
                pe.wait_ge(copied, n + START)
                for k in range(PARTS):
                    kt = half * PARTS + k
                    tr = nc.tensor.transpose(bank[:, k, :], rows[:, i % RING, kt * P:(kt + 1) * P], ident[:])
                tr.then_inc(done, 1)

            def qk(b, g, s, k):
                n = "qk"[s % 2]
                mm = nc.tensor.matmul(ps_side[:], w[n][:, k, g * P:(g + 1) * P],
                                      ht[:, k, s // 2 * BANK:(s // 2 + 1) * BANK],
                                      start=(k == 0), stop=(k == DCH - 1))
                if k == DCH - 1:
                    mm.then_inc(qk_done, 1)

            def values(g, s, half):
                for t in range(half * 2, half * 2 + 2):
                    tok = slice((s * PARTS + t) * P, (s * PARTS + t + 1) * P)
                    for k in range(DCH):
                        mm = nc.tensor.matmul(ps_side[:, t * P:(t + 1) * P], ht[:, k, tok],
                                              w["v"][:, k, g * P:(g + 1) * P], start=(k == 0), stop=(k == DCH - 1))
                if half == 1:
                    mm.then_inc(v_done, 1)

            def turn_ht(s):
                c, k = s // DCH, s % DCH
                for t in range(PARTS):
                    tr = nc.tensor.transpose(ps_side[:, t * P:(t + 1) * P],
                                             xn[:, c * PARTS + t, k * P:(k + 1) * P], ident[:])
                tr.then_inc(ht_turned, 1)

            def project_out(before, u, half):
                if half == 0:
                    pe.wait_ge(heads_normed, before + START)
                t = half
                q0 = u * UNIT_Q + t * P
                lhs = (heads_t[0][:, q0:q0 + P], heads_t[1][:, u % 2, t * P:(t + 1) * P])
                for g in range(PHASES):
                    mm = nc.tensor.matmul(ps_side[:, t * DIM:(t + 1) * DIM], lhs[g], w["o"][:, g, :],
                                          start=(g == 0), stop=(g == PHASES - 1))
                if half == 1:
                    mm.then_inc(o_done, 1)

            def turn_inv(before):
                pe.wait_ge(inv_spread, before + START)
                for t in range(UNIT_TILES):
                    tr = nc.tensor.transpose(ps_side[:, t * P:(t + 1) * P],
                                             inv_wide[:, t].rearrange("p h d -> p (h d)"), ident[:])
                tr.then_inc(inv_turned, 1)

            def heads(n, before, g, half):
                pe.wait_ge((copied_a, copied_b)[half], n + START)
                if half == 0:
                    pe.wait_ge(heads_normed, before - 1 + START)
                for kt in range(half * PARTS, (half + 1) * PARTS):
                    for h in range(PARTS):
                        mm = nc.tensor.matmul(ps_heads[h * HEAD_DIM:(h + 1) * HEAD_DIM, 0:UNIT_Q],
                                              v[g][:, kt, h * HEAD_DIM:(h + 1) * HEAD_DIM],
                                              turned_p[:, h, kt, :], start=(kt == 0), stop=(kt == TILES - 1))
                if half == 1:
                    mm.then_inc(heads_done, 1)

            pe.sem_inc(inv_turned, START)
            pe.wait_ge(ident_ready, 1)
            pe.wait_ge(normed, TILES)
            for s in range(HT_STEPS):
                if s:
                    pe.wait_ge(ht_done, s)
                turn_ht(s)
            pe.wait_ge(weights_ready, 2)
            pe.wait_ge(ht_done, HT_STEPS)
            for s in range(QK_STEPS):
                if s:
                    pe.wait_ge(lo_done, s)
                for k in range(DCH):
                    qk(0, 0, s, k)
            pe.wait_ge(lo_done, QK_STEPS)
            for s in range(V_STEPS):
                if s:
                    pe.wait_ge(v_ready, s)
                values(0, s, 0)
                values(0, s, 1)
            scores(0, 0, False, 1)
            scores(1, 1, False, 1)
            scores(2, 2, True, 1)

            def slot(b, g, i, first, last):
                n, u = row(b, g, i), i // UNIT_ROWS
                for half in range(2):
                    if i % UNIT_ROWS == 0 and not (first and i == 0):
                        heads(n, unit(b, g, u), g if u else 1 - g, half)
                    turn(b, g, i, half)
                m = ahead(g, i, 3)
                if not (last and m >= BATCH_ROWS):
                    if m % ROWS < PARTS:
                        fills = b + (1 if m < BATCH_ROWS else 2)
                    else:
                        fills = None
                    scores(m, row(b, 0, m), True, fills)
                work = side_work(g, i, first, last)
                if work is None:
                    return
                kind, s, part, parts = work
                if part == 0:
                    side_wait(b, g, i, first, last)
                if kind == "inv":
                    turn_inv(unit(b, g, u))
                elif kind == "qk":
                    qk(b, 1 - g, s, part)
                elif kind == "v":
                    values(1 - g, s, part)
                elif kind == "ht":
                    if s == 0:
                        pe.wait_ge(normed, (b + 2) * TILES)
                    turn_ht(s)
                else:
                    project_out(unit(b, g, 0) if g == 0 else unit(b, 1, s) + 1, s, part)

            def tail():
                b, units = BATCH - 1, BATCH * BATCH_UNITS
                for half in range(2):
                    heads(BATCH * BATCH_ROWS, units, 1, half)
                pe.wait_ge(out_ready, BATCH * UNITS - 1)
                turn_inv(units)
                pe.wait_ge(inv_copied, units)
                for half in range(2):
                    project_out(units, UNITS - 1, half)

            slots(pe, slot, tail)


_INS = ["x", "adj", "L0_gnn_Wq", "L0_gnn_bq", "L0_gnn_Wk", "L0_gnn_bk", "L0_gnn_Wv", "L0_gnn_bv",
        "L0_gnn_Wo", "L0_gnn_bo"]


def kernel(**inputs):
    import numpy as _np
    import concourse.bacc as _bacc
    from concourse.bass_utils import run_bass_kernel_spmd as _run

    nc = _bacc.Bacc("TRN2", target_bir_lowering=False, num_devices=1)
    arrays, args = {}, []
    for name in _INS:
        a = _np.ascontiguousarray(inputs[name])
        arrays[f"in_{name}"] = a
        args.append(nc.dram_tensor(f"in_{name}", a.shape, mybir.dt.from_np(a.dtype), kind="ExternalInput").ap())
    args.append(nc.dram_tensor("out_0", (BATCH, TOKENS, DIM), F32, kind="ExternalOutput").ap())
    gnn_kernel(nc, *args)
    r = _run(nc, [arrays], core_ids=[0])
    return r.results[0]["out_0"]
```

```python
from contextlib import ExitStack

import concourse.bass as bass
from concourse import mybir

F32 = mybir.dt.float32
F32R = mybir.dt.float32r
ALU = mybir.AluOpType
ACT = mybir.ActivationFunctionType

P = 128
BANK = 512
BATCH, TOKENS, DIM, HEADS = 8, 1024, 256, 8
HEAD_DIM = DIM // HEADS
PARTS = P // HEAD_DIM
PHASES = HEADS // PARTS
TILES = TOKENS // P
DCH = DIM // P
CHUNKS = TOKENS // BANK
UNIT_TILES = 2
UNIT_Q = UNIT_TILES * P
UNIT_ROWS = UNIT_TILES * PARTS
UNITS = TILES // UNIT_TILES
ROWS = UNITS * UNIT_ROWS
BATCH_ROWS = PHASES * ROWS
BATCH_UNITS = PHASES * UNITS
RING = 4
SCORES_AHEAD, MASK_AHEAD, EXP_AHEAD = 4, 3, 1
ACT_COPIES = (4, 7)

EPS = 1e-5
MASKED = 1e9
START_MIN = 3.0e38

QK_STEPS = 2 * CHUNKS
V_STEPS = TILES * P // BANK
HT_STEPS = DCH * CHUNKS
HEAD_DMAS = 2 * PARTS

PIECES = 4
SIDE_STEPS = (
    (("qk", 0, (1, 1, 2, 2)), ("o", 3, (3, 3, 4, 4)), ("qk", 1, (5, 5, 7, 7)), ("qk", 2, (9, 9, 11, 11)),
     ("qk", 3, (13, 13, 14, 14)), ("v", 0, (17, 18, 19, 19)), ("v", 1, (21, 21, 22, 22)),
     ("ht", 0, (26, 26, 26, 26)), ("ht", 1, (27, 27, 27, 27)), ("ht", 2, (29, 29, 29, 29)),
     ("ht", 3, (30, 30, 30, 30))),
    (("v", 0, (1, 1, 3, 3)), ("qk", 0, (5, 5, 6, 6)), ("qk", 1, (8, 8, 8, 8)), ("qk", 2, (10, 10, 11, 11)),
     ("qk", 3, (13, 13, 14, 14)), ("v", 1, (16, 16, 17, 17)), ("o", 0, (18, 18, 20, 20)),
     ("o", 1, (22, 22, 25, 25)), ("o", 2, (27, 29, 29, 29))),
)
SIDE = [{i: (kind, s, [n for n in range(PIECES) if at[n] == i]) for kind, s, at in steps for i in at}
        for steps in SIDE_STEPS]
START_STEPS = (("ht", 0), ("ht", 1), ("qk", 0), ("ht", 2), ("ht", 3), ("qk", 1), ("qk", 2), ("qk", 3),
               ("v", 0), ("v", 1))
HEAD = 7
INV_ROW, NORM_ROW = 1, 2
STATS = {8: (0, 1, 2, 3), 16: (4, 5, 6, 7)}
NORM_UNIT = 2


def side_work(g, i, first, last):
    work = SIDE[g].get(i)
    if work is None:
        return None
    kind = work[0]
    if first and g == 0 and i < HEAD and kind == "o":
        return None
    if last and (kind == "ht" or g == 1 and kind in ("qk", "v")):
        return None
    return work


def gnn_kernel(nc, x, adj, Wq, bq, Wk, bk, Wv, bv, Wo, bo, out):
    SCALE = float(HEAD_DIM) ** -0.5
    x_v = x.rearrange("b (t p) d -> b p t d", p=P)
    out_v = out.rearrange("b (t p) d -> b p t d", p=P)
    adj_v = adj.rearrange("(t p) k -> p t k", p=P)

    with ExitStack() as ctx:
        def sb(name, shape, dt=F32):
            return ctx.enter_context(nc.sbuf_tensor(name, shape, dt))

        def pb(name, shape, dt=F32):
            return ctx.enter_context(nc.psum_tensor(name, shape, dt))

        def sem(name):
            return ctx.enter_context(nc.semaphore(name))

        mask = sb("mask", [P, TILES, TOKENS])
        q_stack = [sb(f"q_stack{g}", [P, PARTS, TOKENS], F32R) for g in range(PHASES)]
        k_stack = [sb(f"k_stack{g}", [P, PARTS, TOKENS], F32R) for g in range(PHASES)]
        rows = sb("rows", [P, RING, TOKENS])
        turned_p = sb("turned_p", [P, PARTS, TILES, UNIT_Q])
        hi = [sb(f"{n}_hi", [P, TOKENS], F32R) for n in "qk"]
        lo = [sb(f"{n}_lo", [P, TOKENS], F32R) for n in "qk"]
        ht = sb("ht", [P, DCH, TOKENS])
        xn = sb("xn", [P, TILES, DIM])
        v = [sb(f"v{g}", [P, TILES, P]) for g in range(PHASES)]
        w = {n: sb(f"w{n}", [P, DCH, DIM]) for n in "qkvo"}
        heads_t = [sb("heads_t0", [P, TOKENS]), sb("heads_t1", [P, 2, UNIT_Q])]
        res = sb("res", [P, 2, UNIT_TILES, DIM])
        inv_wide = sb("inv_wide", [P, UNIT_TILES, PARTS, HEAD_DIM])
        inv_t = sb("inv_t", [P, UNIT_Q])
        ident = sb("ident", [P, P])
        bv_row = sb("bv_row", [P, DIM])
        bo_row = sb("bo_row", [P, DIM])
        bias = {n: sb(f"b{n}_col", [P, PHASES]) for n in "qk"}
        row_min = sb("row_min", [P, RING])
        row_sum = sb("row_sum", [P, 2, UNIT_ROWS])
        row_inv = sb("row_inv", [P, UNIT_ROWS])
        stats = sb("stats", [P, TILES, 6])
        mean_var = sb("mean_var", [P, TILES, 2])
        ln = {n: sb(f"ln_{n}", [P, TILES]) for n in ("neg_mean", "var", "power", "rstd", "t0", "t1", "t2")}

        ps_scores = [pb(f"ps_scores{i}", [P, TOKENS]) for i in range(2)]
        ps_turn = [pb(f"ps_turn{i}", [P, PARTS, P]) for i in range(2)]
        ps_heads = pb("ps_heads", [P, BANK])
        ps_side = pb("ps_side", [P, BANK])

        start_banks = [ps_side[:], ps_heads[:]] + [ps_turn[i][:].rearrange("p k n -> p (k n)") for i in range(2)]
        HT_BANKS, QK_BANKS, V_BANKS = start_banks[0:2], start_banks[2:4], start_banks[0:2]

        START = 1
        LN_STEPS = 7
        qk_weights_in = sem("qk_weights_in")
        weights_in = sem("weights_in")
        mask_in = [sem(f"mask_in{i}") for i in range(2)]
        x_start_in = sem("x_start_in")
        x_in = sem("x_in")
        res_in = [sem(f"res_in{i}") for i in range(2)]
        stacked = [[sem(f"stacked{g}_{h}") for h in range(PARTS)] for g in range(PHASES)]
        start_stacked = [sem(f"start_stacked{h}") for h in range(PARTS)]
        out_stored = sem("out_stored")
        weights_ready = sem("weights_ready")
        mask_ready = sem("mask_ready")
        ident_ready = sem("ident_ready")
        stats_done = sem("stats_done")
        moments_done = sem("moments_done")
        ln_chain = sem("ln_chain")
        normed = sem("normed")
        scores_done = sem("scores_done")
        masked = sem("masked")
        exp_done = sem("exp_done")
        turn_a = sem("turn_a")
        turn_b = sem("turn_b")
        copied_a = sem("copied_a")
        copied_b = sem("copied_b")
        heads_done = sem("heads_done")
        inv_done = sem("inv_done")
        inv_spread = sem("inv_spread")
        inv_turned = sem("inv_turned")
        inv_copied = sem("inv_copied")
        heads_normed = sem("heads_normed")
        ht_turned = sem("ht_turned")
        ht_done = sem("ht_done")
        qk_done = sem("qk_done")
        hi_done = sem("hi_done")
        lo_done = sem("lo_done")
        v_done = sem("v_done")
        v_ready = sem("v_ready")
        o_done = sem("o_done")
        res_ready = sem("res_ready")
        out_ready = sem("out_ready")

        def row(b, g, i):
            return b * BATCH_ROWS + (g * ROWS + i)

        def unit(b, g, u):
            return b * BATCH_UNITS + (g * UNITS + u)

        def ahead(g, i, k):
            return g * ROWS + i + k

        def qk_step(b, g, s):
            return b * (2 * QK_STEPS) + (g * QK_STEPS + s)

        def v_step(b, g, s):
            return b * (2 * V_STEPS) + (g * V_STEPS + s)

        def held(eng, count):
            return count if isinstance(count, int) else eng.snap(eng.to_reg(count))

        def slots(eng, slot, tail):
            def rest_of(b, last):
                for g in range(PHASES):
                    for i in range(HEAD if g == 0 else 0, ROWS):
                        slot(b, g, i, False, last)

            for i in range(HEAD):
                slot(0, 0, i, True, False)
            with eng.Fori(0, BATCH - 1) as b:
                rest_of(b, False)
                for i in range(HEAD):
                    slot(b + 1, 0, i, False, False)
            rest_of(BATCH - 1, True)
            tail()

        POOL_COPIES = 3

        def stack_count(g, fills):
            return (fills * HEAD_DMAS - (POOL_COPIES if g == 0 else 0)) * 16

        def stack_head(eng, done, g, h, n, copies=range(PARTS)):
            dst, parts = {"q": (q_stack[g], (hi[0], lo[0], hi[0], lo[0])),
                          "k": (k_stack[g], (hi[1], hi[1], lo[1], lo[1]))}[n]
            for r in copies:
                eng.dma_start(dst[r * HEAD_DIM:(r + 1) * HEAD_DIM, h, :].bitcast(F32),
                              parts[r][h * HEAD_DIM:(h + 1) * HEAD_DIM, :].bitcast(F32)
                              ).then_inc(done, 16)

        block = ctx.enter_context(nc.Block())

        @block.sync
        def _(sp):
            def load_x(b):
                sp.dma_start(xn[:], x_v[b]).then_inc(x_in, 16)

            def load_res(b, u):
                sp.dma_start(res[:, u % 2], x_v[b, :, u * UNIT_TILES:(u + 1) * UNIT_TILES, :]
                             ).then_inc(res_in[u % 2], 16)

            def stack(bg, g, rows_before):
                sp.wait_ge(scores_done, rows_before)
                sp.wait_ge(lo_done, qk_step(bg, g, QK_STEPS - 1) + 1)
                for h in range(PARTS):
                    stack_head(sp, stacked[g][h], g, h, "q")
                    stack_head(sp, stacked[g][h], g, h, "k")

            def load_weights(n, src, done):
                sp.dma_start(w[n][:], src.rearrange("(c p) n -> p c n", p=P)).then_inc(done, 16)

            sp.dma_start(xn[:, 0:PARTS, :], x_v[0, :, 0:PARTS, :]).then_inc(x_start_in, 16)
            sp.dma_start(xn[:, PARTS:TILES, :], x_v[0, :, PARTS:TILES, :]).then_inc(x_in, 16)
            for n, src, b_src in (("q", Wq, bq), ("k", Wk, bk)):
                load_weights(n, src, qk_weights_in)
                sp.dma_start(bias[n][:], b_src.rearrange("(g p) -> p g", p=P), allow_slow_non_contiguous=True
                             ).then_inc(qk_weights_in, 16)
            sp.dma_start(mask[:, 0, :], adj_v[:, 0, :]).then_inc(mask_in[0], 16)
            for n, src, row_t, b_src in (("v", Wv, bv_row, bv), ("o", Wo, bo_row, bo)):
                load_weights(n, src, weights_in)
                sp.dma_start(row_t[:], b_src.partition_broadcast(P)).then_inc(weights_in, 16)
            sp.dma_start(mask[:, 1:TILES, :], adj_v[:, 1:TILES, :]).then_inc(mask_in[1], 16)
            load_res(0, 0)
            load_res(0, 1)
            sp.wait_ge(lo_done, QK_STEPS - 1)
            for h in range(PARTS):
                stack_head(sp, stacked[0][h], 0, h, "q", range(POOL_COPIES, PARTS))
            sp.wait_ge(lo_done, QK_STEPS)
            for h in range(PARTS):
                stack_head(sp, stacked[0][h], 0, h, "k")

            sp.wait_ge(ht_turned, HT_STEPS)
            load_x(1)

            def body(b, left):
                stack(b, 1, row(b, 0, 0) + 1)
                if left > 1:
                    sp.wait_ge(ht_turned, b * HT_STEPS + 2 * HT_STEPS)
                    load_x(b + 2)
                if left > 0:
                    stack(b + 1, 0, row(b, 1, 0))
                for u in range(UNITS):
                    sp.wait_ge(out_ready, b * UNITS + (u + 1))
                    sp.dma_start(out_v[b, :, u * UNIT_TILES:(u + 1) * UNIT_TILES, :], res[:, u % 2]
                                 ).then_inc(out_stored, 16)
                    if u + 2 < UNITS or left > 0:
                        sp.wait_ge(out_stored, (b * UNITS + (u + 1)) * 16)
                        load_res(*((b, u + 2) if u + 2 < UNITS else (b + 1, u + 2 - UNITS)))

            with sp.Fori(0, BATCH - 2) as b:
                body(b, 2)
            body(BATCH - 2, 1)
            body(BATCH - 1, 0)
            sp.wait_ge(out_stored, BATCH * UNITS * 16)

        @block.gpsimd
        def _(pool):
            pool.sem_inc(inv_spread, START)
            pool.memset(ident[:], 0.0).then_inc(turn_b, RING)
            pool.wait_ge(turn_b, RING)
            pool.affine_select(out=ident[:], in_=ident[:], compare_op=ALU.not_equal, fill=1.0, base=0,
                               pattern=[[-1, P]], channel_multiplier=1).then_inc(ident_ready, 1)
            pool.memset(ln["power"][:], -0.5).then_inc(ln_chain, 1)

            def own():
                pool.wait_ge(ident_ready, 1)

            RES_UNITS = {(0, 3): 0, (1, 0): 1, (1, 2): 2, (1, 3): 3}

            def deviations(base, tiles, moments_count):
                count = held(pool, moments_count)
                own()
                pool.wait_ge(moments_done, count)
                mean, var = mean_var[:, tiles, 0], mean_var[:, tiles, 1]
                neg_mean, var_eps, rstd, t0, t1, t2 = (ln[n][:, tiles] for n in
                                                       ("neg_mean", "var", "rstd", "t0", "t1", "t2"))
                pool.tensor_scalar(neg_mean, mean, -1.0, None, ALU.mult).then_inc(ln_chain, 1)
                pool.tensor_scalar(var_eps, var, EPS, None, ALU.add).then_inc(ln_chain, 1)
                pool.wait_ge(ln_chain, base + 2)
                pool.tensor_tensor(t0, var_eps, ln["power"][:, tiles], ALU.pow).then_inc(ln_chain, 1)
                pool.wait_ge(ln_chain, base + 3)
                pool.tensor_tensor(t1, t0, t0, ALU.mult).then_inc(ln_chain, 1)
                pool.wait_ge(ln_chain, base + 4)
                pool.tensor_tensor(t2, t1, var_eps, ALU.mult).then_inc(ln_chain, 1)
                count = held(pool, base + 5)
                own()
                pool.wait_ge(ln_chain, count)
                pool.tensor_scalar(t1, t2, -0.5, 1.5, ALU.mult, ALU.add).then_inc(ln_chain, 1)
                pool.wait_ge(ln_chain, base + 6)
                pool.tensor_tensor(rstd, t0, t1, ALU.mult).then_inc(ln_chain, 1)

            def norm(b):
                base = b * LN_STEPS + (LN_STEPS + 1)
                deviations(base, slice(0, TILES), b * TILES + TILES)
                count = held(pool, base + LN_STEPS)
                own()
                pool.wait_ge(ln_chain, count)
                for t in range(TILES):
                    pool.tensor_scalar(xn[:, t, :], xn[:, t, :], ln["neg_mean"][:, t:t + 1],
                                       ln["rstd"][:, t:t + 1], ALU.add, ALU.mult).then_inc(normed, 1)

            deviations(1, slice(0, PARTS), PARTS)
            deviations(1 + LN_STEPS, slice(PARTS, TILES), TILES)
            pool.wait_ge(lo_done, QK_STEPS - 1)
            for h in range(PARTS):
                stack_head(pool, start_stacked[h], 0, h, "q", range(POOL_COPIES))
            pool.wait_ge(weights_in, 4 * 16)

            def body(b, last):
                for g in range(PHASES):
                    for u in range(UNITS):
                        count = held(pool, unit(b, g, u) + 1)
                        own()
                        pool.wait_ge(inv_done, count)
                        pool.wait_ge(inv_turned, count)
                        pool.tensor_copy(inv_wide[:], row_inv[:].rearrange("p (t h) -> p t h", h=PARTS)
                                         .unsqueeze(3).to_broadcast([P, UNIT_TILES, PARTS, HEAD_DIM])
                                         ).then_inc(inv_spread, 1)
                        if g == 0 and u == NORM_UNIT and not last:
                            norm(b + 1)
                        k = RES_UNITS.get((g, u))
                        if k is not None:
                            pool.wait_ge(res_in[k % 2], (b * (UNITS // 2) + (k // 2 + 1)) * 16)
                            pool.tensor_tensor(res[:, k % 2], res[:, k % 2],
                                               bo_row[:].unsqueeze(1).to_broadcast([P, UNIT_TILES, DIM]),
                                               ALU.add).then_inc(res_ready, 1)

            with pool.Fori(0, BATCH - 1) as b:
                body(b, False)
            body(BATCH - 1, True)

        @block.scalar
        def _(act):
            def exp(m, n):
                act.wait_ge(masked, n + 1)
                u, j = m // UNIT_ROWS, m % UNIT_ROWS
                nc.scalar.activation(rows[:, m % RING, :], rows[:, m % RING, :], ACT.Exp,
                                     bias=row_min[:, m % RING:m % RING + 1], scale=-1.0,
                                     accum_out=row_sum[:, u % 2, j:j + 1]).then_inc(exp_done, 1)

            def copy_a(b, g, i):
                act.wait_ge(turn_a, row(b, g, i) + 1)
                t, h = i // PARTS % UNIT_TILES, i % PARTS
                nc.scalar.activation(turned_p[:, h, 0:PARTS, t * P:(t + 1) * P], ps_turn[0][:], ACT.Copy
                                     ).then_inc(copied_a, 1)

            def copy_b(b, g, i):
                act.wait_ge(turn_b, row(b, g, i) + (RING + 1))
                t, h = i // PARTS % UNIT_TILES, i % PARTS
                nc.scalar.activation(turned_p[:, h, PARTS:TILES, t * P:(t + 1) * P], ps_turn[1][:], ACT.Copy
                                     ).then_inc(copied_b, 1)

            def high_part(b, g, s, bank=ps_side[:]):
                act.wait_ge(qk_done, qk_step(b, g, s) + 1)
                nc.scalar.activation(hi[s % 2][:, s // 2 * BANK:(s // 2 + 1) * BANK], bank, ACT.Identity,
                                     bias=bias["qk"[s % 2]][:, g:g + 1]).then_inc(hi_done, 1)

            def copy_ht(b, s, bank=ps_side[:]):
                act.wait_ge(ht_turned, b * HT_STEPS + (s + 1))
                c, k = s // DCH, s % DCH
                nc.scalar.activation(ht[:, k, c * BANK:(c + 1) * BANK], bank, ACT.Relu).then_inc(ht_done, 1)

            def copy_inv(turned):
                act.wait_ge(inv_turned, turned + START)
                act.wait_ge(heads_normed, turned - 1 + START)
                nc.scalar.activation(inv_t[:], ps_heads[:, UNIT_Q:], ACT.Copy).then_inc(inv_copied, 1)

            act.sem_inc(copied_a, START)
            act.wait_ge(qk_weights_in, 4 * 16)
            nc.scalar.activation(w["q"][:], w["q"][:], ACT.Copy, scale=-SCALE).then_inc(weights_ready, 1)
            nc.scalar.activation(bias["q"][:], bias["q"][:], ACT.Copy, scale=-SCALE).then_inc(weights_ready, 1)
            for kind, s in START_STEPS:
                if kind == "ht":
                    copy_ht(0, s, HT_BANKS[s % 2])
                elif kind == "qk":
                    act.wait_ge(weights_ready, 2)
                    high_part(0, 0, s, QK_BANKS[s % 2])
            for m in range(EXP_AHEAD):
                exp(m, m)

            def slot(b, g, i, first, last):
                m = ahead(g, i, EXP_AHEAD)
                if not (last and m >= BATCH_ROWS):
                    exp(m, row(b, 0, m))
                kind, s, pieces = side_work(g, i - 1, first, last) or (None, 0, [])
                done = PIECES - 1 in pieces
                if i % UNIT_ROWS == INV_ROW + 1 and not (first and i < HEAD):
                    copy_inv(unit(b, g, i // UNIT_ROWS))
                if kind == "ht" and done:
                    copy_ht(b + 1, s)
                if kind == "qk" and done:
                    if s == 0:
                        for h in range(PARTS):
                            act.wait_ge(stacked[g][h], stack_count(g, b + 1))
                    high_part(*((b, 1) if g == 0 else (b + 1, 0)), s)
                copy_a(b, g, i)
                if i % UNIT_ROWS in ACT_COPIES:
                    copy_b(b, g, i)

            def tail():
                copy_inv(BATCH * BATCH_UNITS)

            slots(act, slot, tail)

        @block.vector
        def _(dve):
            def mask_row(m, n, qt):
                count = held(dve, n + 1)
                dve.wait_ge(mask_ready, 2)
                dve.wait_ge(scores_done, count)
                dve.wait_ge(turn_b, count)
                nc.vector.tensor_tensor_reduce(out=rows[:, m % RING, :], in0=ps_scores[m % 2][:],
                                               in1=mask[:, qt, :], scale=1.0, scalar=START_MIN,
                                               op0=ALU.add, op1=ALU.min,
                                               accum_out=row_min[:, m % RING:m % RING + 1]).then_inc(masked, 1)

            def tile_of(m):
                return m % ROWS // PARTS

            def copy_b(b, g, i):
                dve.wait_ge(turn_b, row(b, g, i) + (RING + 1))
                t, h = i // PARTS % UNIT_TILES, i % PARTS
                nc.vector.tensor_copy(turned_p[:, h, PARTS:TILES, t * P:(t + 1) * P], ps_turn[1][:]
                                      ).then_inc(copied_b, 1)

            def low_part(b, g, s, bank=ps_side[:]):
                dve.wait_ge(hi_done, qk_step(b, g, s) + 1)
                cols = slice(s // 2 * BANK, (s // 2 + 1) * BANK)
                nc.vector.scalar_tensor_tensor(out=lo[s % 2][:, cols], in0=bank,
                                               scalar=bias["qk"[s % 2]][:, g:g + 1],
                                               in1=hi[s % 2][:, cols].bitcast(F32),
                                               op0=ALU.add, op1=ALU.subtract).then_inc(lo_done, 1)

            def copy_v(b, g, s, bank=ps_side[:]):
                dve.wait_ge(v_done, v_step(b, g, s) + 1)
                nc.vector.tensor_tensor(v[g][:, s * PARTS:(s + 1) * PARTS, :],
                                        bank.rearrange("p (t n) -> p t n", n=P),
                                        bv_row[:, g * P:(g + 1) * P].unsqueeze(1).to_broadcast([P, PARTS, P]),
                                        ALU.add).then_inc(v_ready, 1)

            def moments(b, t):
                if isinstance(b, int) and t == 0:
                    dve.wait_ge(x_start_in, 16)
                elif isinstance(b, int) and t == PARTS or t == 0:
                    dve.wait_ge(x_in, (b + 1) * 16)
                nc.vector.bn_stats(stats[:, t, :], xn[:, t, :]).then_inc(stats_done, 1)
                count = held(dve, b * TILES + (t + 1))
                dve.wait_ge(x_in, 16)
                dve.wait_ge(stats_done, count)
                nc.vector.bn_aggr(mean_var[:, t, :], stats[:, t, :]).then_inc(moments_done, 1)

            def invert(before, u):
                dve.wait_ge(exp_done, before * UNIT_ROWS)
                dve.wait_ge(inv_spread, before - 1 + START)
                nc.vector.reciprocal(row_inv[:], row_sum[:, u % 2, :]).then_inc(inv_done, 1)

            def norm_heads(before, g, u):
                dve.wait_ge(inv_copied, before)
                dve.wait_ge(heads_done, before)
                dst = heads_t[0][:, u * UNIT_Q:(u + 1) * UNIT_Q] if g == 0 else heads_t[1][:, u % 2, :]
                nc.vector.tensor_tensor(dst, ps_heads[:, 0:UNIT_Q], inv_t[:], ALU.mult
                                        ).then_inc(heads_normed, 1)

            def finish(count, u):
                dve.wait_ge(o_done, count)
                dve.wait_ge(res_ready, count)
                nc.vector.tensor_tensor(res[:, u % 2], ps_side[:].rearrange("p (t d) -> p t d", d=DIM),
                                        res[:, u % 2], ALU.add).then_inc(out_ready, 1)

            dve.sem_inc(copied_b, START)
            dve.sem_inc(heads_normed, START)
            for t in range(TILES):
                moments(0, t)
            for t in range(TILES):
                dve.wait_ge(ln_chain, 1 + (t // PARTS + 1) * LN_STEPS)
                nc.vector.tensor_scalar(xn[:, t, :], xn[:, t, :], ln["neg_mean"][:, t:t + 1],
                                        ln["rstd"][:, t:t + 1], ALU.add, ALU.mult).then_inc(normed, 1)
            dve.wait_ge(mask_in[0], 16)
            nc.vector.tensor_scalar(mask[:, 0, :], mask[:, 0, :], 1.0, -MASKED, ALU.subtract, ALU.mult
                                    ).then_inc(mask_ready, 1)
            dve.wait_ge(weights_ready, 2)
            for s in range(QK_STEPS):
                low_part(0, 0, s, QK_BANKS[s % 2])
            dve.wait_ge(weights_in, 4 * 16)
            for s in range(V_STEPS):
                copy_v(0, 0, s, V_BANKS[s])
            dve.wait_ge(mask_in[1], 16)
            nc.vector.tensor_scalar(mask[:, 1:TILES, :], mask[:, 1:TILES, :], 1.0, -MASKED, ALU.subtract, ALU.mult
                                    ).then_inc(mask_ready, 1)
            for m in range(MASK_AHEAD):
                mask_row(m, m, 0)

            def slot(b, g, i, first, last):
                m = ahead(g, i, MASK_AHEAD)
                if not (last and m >= BATCH_ROWS):
                    mask_row(m, row(b, 0, m), tile_of(m))
                kind, s, pieces = side_work(g, i - 1, first, last) or (None, 0, [])
                done = PIECES - 1 in pieces
                if kind in ("qk", "v") and done:
                    {"qk": low_part, "v": copy_v}[kind](*((b, 1) if g == 0 else (b + 1, 0)), s)
                if kind == "o" and done:
                    finish(b * UNITS + (0 if g == 0 else s + 1), s)
                if g == 0 and not last:
                    for t in STATS.get(i, ()):
                        moments(b + 1, t)
                u = i // UNIT_ROWS
                if not (first and i < HEAD):
                    pg, pu = (g, u - 1) if u else (1 - g, UNITS - 1)
                    if i % UNIT_ROWS == 0:
                        invert(unit(b, g, u), pu)
                    if i % UNIT_ROWS == NORM_ROW:
                        norm_heads(unit(b, g, u), pg, pu)
                if i % UNIT_ROWS not in ACT_COPIES:
                    copy_b(b, g, i)

            def tail():
                units = BATCH * BATCH_UNITS
                invert(units, UNITS - 1)
                norm_heads(units, 1, UNITS - 1)
                finish(BATCH * UNITS, UNITS - 1)

            slots(dve, slot, tail)

        @block.tensor
        def _(pe):
            def side_wait(b, g, i, first, last):
                pg, pi = g, i - 1
                while pi >= 0 or pg == 1:
                    if pi < 0:
                        pg, pi = 0, ROWS - 1
                    if side_work(pg, pi, first, last) is not None:
                        break
                    pi -= 1
                if pi < 0:
                    if first:
                        pe.wait_ge(v_ready, V_STEPS)
                    else:
                        pe.wait_ge(out_ready, b * UNITS - 1)
                    return
                kind, s, _ = side_work(pg, pi, first, last)
                nb, ng = (b, 1) if pg == 0 else (b + 1, 0)
                if kind == "qk":
                    pe.wait_ge(lo_done, qk_step(nb, ng, s) + 1)
                elif kind == "v":
                    pe.wait_ge(v_ready, v_step(nb, ng, s) + 1)
                elif kind == "ht":
                    pe.wait_ge(ht_done, (b + 1) * HT_STEPS + (s + 1))
                else:
                    pe.wait_ge(out_ready, b * UNITS + (0 if pg == 0 else s + 1))

            def scores(m, n, wait_free, fills):
                g, i = m // ROWS % PHASES, m % ROWS
                qt, h = i // PARTS, i % PARTS
                if fills is not None:
                    pe.wait_ge(stacked[g][h], stack_count(g, fills))
                    if isinstance(fills, int) and fills == 1 and g == 0:
                        pe.wait_ge(start_stacked[h], POOL_COPIES * 16)
                if wait_free:
                    pe.wait_ge(masked, n - 1)
                for c in range(CHUNKS):
                    mm = nc.tensor.matmul(ps_scores[m % 2][:, c * BANK:(c + 1) * BANK],
                                          q_stack[g][:, h, qt * P:(qt + 1) * P],
                                          k_stack[g][:, h, c * BANK:(c + 1) * BANK], start=True, stop=True)
                mm.then_inc(scores_done, 1)

            def turn(b, g, i, half):
                n = row(b, g, i)
                bank, done, copied = ((ps_turn[0], turn_a, copied_a), (ps_turn[1], turn_b, copied_b))[half]
                if half == 0:
                    pe.wait_ge(exp_done, n + 1)
                pe.wait_ge(copied, n + START)
                for k in range(PARTS):
                    kt = half * PARTS + k
                    tr = nc.tensor.transpose(bank[:, k, :], rows[:, i % RING, kt * P:(kt + 1) * P], ident[:])
                tr.then_inc(done, 1)

            def qk(g, s, piece, bank=ps_side[:]):
                n, half, k = "qk"[s % 2], piece // DCH, piece % DCH
                cols = slice(half * BANK // 2, (half + 1) * BANK // 2)
                mm = nc.tensor.matmul(bank[:, cols], w[n][:, k, g * P:(g + 1) * P],
                                      ht[:, k, s // 2 * BANK:(s // 2 + 1) * BANK][:, cols],
                                      start=(k == 0), stop=(k == DCH - 1))
                if piece == PIECES - 1:
                    mm.then_inc(qk_done, 1)

            def values(g, s, t, bank=ps_side[:]):
                tok = slice((s * PARTS + t) * P, (s * PARTS + t + 1) * P)
                for k in range(DCH):
                    mm = nc.tensor.matmul(bank[:, t * P:(t + 1) * P], ht[:, k, tok],
                                          w["v"][:, k, g * P:(g + 1) * P], start=(k == 0), stop=(k == DCH - 1))
                if t == PIECES - 1:
                    mm.then_inc(v_done, 1)

            def turn_ht(s, t, bank=ps_side[:]):
                c, k = s // DCH, s % DCH
                tr = nc.tensor.transpose(bank[:, t * P:(t + 1) * P], xn[:, c * PARTS + t, k * P:(k + 1) * P], ident[:])
                if t == PIECES - 1:
                    tr.then_inc(ht_turned, 1)

            def project_out(before, u, piece):
                t, g = piece // PHASES, piece % PHASES
                if piece == 0:
                    pe.wait_ge(heads_normed, before + START)
                q0 = u * UNIT_Q + t * P
                lhs = (heads_t[0][:, q0:q0 + P], heads_t[1][:, u % 2, t * P:(t + 1) * P])[g]
                mm = nc.tensor.matmul(ps_side[:, t * DIM:(t + 1) * DIM], lhs, w["o"][:, g, :],
                                      start=(g == 0), stop=(g == PHASES - 1))
                if piece == PIECES - 1:
                    mm.then_inc(o_done, 1)

            def turn_inv(before):
                pe.wait_ge(inv_spread, before + START)
                for t in range(UNIT_TILES):
                    tr = nc.tensor.transpose(ps_heads[:, UNIT_Q + t * P:UNIT_Q + (t + 1) * P],
                                             inv_wide[:, t].rearrange("p h d -> p (h d)"), ident[:])
                tr.then_inc(inv_turned, 1)

            def heads(n, before, g, half):
                pe.wait_ge((copied_a, copied_b)[half], n + START)
                if half == 0:
                    pe.wait_ge(heads_normed, before - 1 + START)
                for kt in range(half * PARTS, (half + 1) * PARTS):
                    for h in range(PARTS):
                        mm = nc.tensor.matmul(ps_heads[h * HEAD_DIM:(h + 1) * HEAD_DIM, 0:UNIT_Q],
                                              v[g][:, kt, h * HEAD_DIM:(h + 1) * HEAD_DIM],
                                              turned_p[:, h, kt, :], start=(kt == 0), stop=(kt == TILES - 1))
                if half == 1:
                    mm.then_inc(heads_done, 1)

            pe.sem_inc(inv_turned, START)
            pe.wait_ge(ident_ready, 1)
            for kind, s in START_STEPS:
                for piece in range(PIECES):
                    if kind == "ht":
                        if s % DCH == 0:
                            pe.wait_ge(normed, s // DCH * PARTS + piece + 1)
                        turn_ht(s, piece, HT_BANKS[s % 2])
                    elif kind == "qk":
                        if piece == 0:
                            pe.wait_ge(weights_ready, 1)
                            pe.wait_ge(ht_done, (s // DCH + 1) * DCH)
                            if s >= 2:
                                pe.wait_ge(lo_done, s - 1)
                        qk(0, s, piece, QK_BANKS[s % 2])
                    else:
                        if piece == 0:
                            pe.wait_ge(weights_in, 4 * 16)
                        values(0, s, piece, V_BANKS[s])
            pe.wait_ge(lo_done, QK_STEPS)
            for m in range(SCORES_AHEAD):
                scores(m, m, m >= 2, 1)

            def slot(b, g, i, first, last):
                n, u = row(b, g, i), i // UNIT_ROWS
                for half in range(2):
                    if i % UNIT_ROWS == 0 and not (first and i == 0):
                        heads(n, unit(b, g, u), g if u else 1 - g, half)
                    turn(b, g, i, half)
                m = ahead(g, i, SCORES_AHEAD)
                if not (last and m >= BATCH_ROWS):
                    if m % ROWS < PARTS:
                        fills = b + (1 if m < BATCH_ROWS else 2)
                    else:
                        fills = None
                    scores(m, row(b, 0, m), True, fills)
                if i % UNIT_ROWS == INV_ROW and not (first and i < HEAD):
                    turn_inv(unit(b, g, u))
                work = side_work(g, i, first, last)
                if work is None:
                    return
                kind, s, pieces = work
                if 0 in pieces:
                    side_wait(b, g, i, first, last)
                    if kind == "ht" and s % DCH == 0:
                        pe.wait_ge(normed, (b + 1) * TILES + (s // DCH + 1) * PARTS)
                for piece in pieces:
                    if kind == "qk":
                        qk(1 - g, s, piece)
                    elif kind == "v":
                        values(1 - g, s, piece)
                    elif kind == "ht":
                        turn_ht(s, piece)
                    else:
                        project_out(unit(b, g, 0) if g == 0 else unit(b, 1, s) + 1, s, piece)

            def tail():
                b, units = BATCH - 1, BATCH * BATCH_UNITS
                for half in range(2):
                    heads(BATCH * BATCH_ROWS, units, 1, half)
                turn_inv(units)
                pe.wait_ge(out_ready, BATCH * UNITS - 1)
                for piece in range(PIECES):
                    project_out(units, UNITS - 1, piece)

            slots(pe, slot, tail)


_INS = ["x", "adj", "L0_gnn_Wq", "L0_gnn_bq", "L0_gnn_Wk", "L0_gnn_bk", "L0_gnn_Wv", "L0_gnn_bv",
        "L0_gnn_Wo", "L0_gnn_bo"]


def kernel(**inputs):
    import numpy as _np
    import concourse.bacc as _bacc
    from concourse.bass_utils import run_bass_kernel_spmd as _run

    nc = _bacc.Bacc("TRN2", target_bir_lowering=False, num_devices=1)
    arrays, args = {}, []
    for name in _INS:
        a = _np.ascontiguousarray(inputs[name])
        arrays[f"in_{name}"] = a
        args.append(nc.dram_tensor(f"in_{name}", a.shape, mybir.dt.from_np(a.dtype), kind="ExternalInput").ap())
    args.append(nc.dram_tensor("out_0", (BATCH, TOKENS, DIM), F32, kind="ExternalOutput").ap())
    gnn_kernel(nc, *args)
    r = _run(nc, [arrays], core_ids=[0])
    return r.results[0]["out_0"]
```
